# Optimizing a Trainium2 kernel written in Bass

```python
import numpy as np
import jax
import jax.numpy as jnp

def _softmax(x, axis=-1):
    return jax.nn.softmax(x, axis=axis)

def _gelu(x):
    return jax.nn.gelu(x, approximate=True)

def _silu(x):
    return jax.nn.silu(x)

def _sigmoid(x):
    return jax.nn.sigmoid(x)

def _layernorm(x, axis=-1, eps=1e-05):
    m = jnp.mean(x, axis=axis, keepdims=True)
    v = jnp.var(x, axis=axis, keepdims=True)
    return (x - m) / jnp.sqrt(v + eps)

def _scatter_add(tgt, idx, src, axis=0):
    return tgt.at[idx].add(src)

def _segment_sum(src, seg, n):
    return jax.ops.segment_sum(src, seg, n)
kernel_name = 'mk_prb_d1_jaxref_r8_cda484'

def setup_inputs(seed: int=0):
    np.random.seed(seed)
    _w = jnp.asarray

    def _L0_attn_setup():
        import math
        import jax, jax.numpy as jnp
        import numpy as np
        DIM = 128
        N_HEADS = 16
        HEAD_DIM = DIM // N_HEADS
        MAX_SEQ_LEN = 512
        ROPE_BASE = 10000.0

        def _rope_tables(seq_len):
            inv_freq = 1.0 / ROPE_BASE ** (jnp.arange(0, HEAD_DIM, 2, dtype=jnp.float32) / HEAD_DIM)
            t = jnp.arange(seq_len, dtype=jnp.float32)
            freqs = jnp.outer(t, inv_freq)
            return (jnp.cos(freqs), jnp.sin(freqs))

        def _rotate_half(x):
            x1 = x[..., 0::2]
            x2 = x[..., 1::2]
            return jnp.stack([-x2, x1], axis=-1).reshape(x.shape)

        def _apply_rope(xq, xk, cos, sin):
            cos = jnp.repeat(cos, 2, axis=-1)[None, None]
            sin = jnp.repeat(sin, 2, axis=-1)[None, None]
            xq_out = xq * cos + _rotate_half(xq) * sin
            xk_out = xk * cos + _rotate_half(xk) * sin
            return (xq_out, xk_out)
        key = jax.random.key(seed)
        kx, kq, kk, kv, ko = jax.random.split(key, 5)
        B, S = (1, 512)
        x = jax.random.normal(kx, (B, S, DIM), dtype=jnp.float32)
        scale = 0.02
        Wq = jax.random.normal(kq, (DIM, DIM), dtype=jnp.float32) * scale
        Wk = jax.random.normal(kk, (DIM, DIM), dtype=jnp.float32) * scale
        Wv = jax.random.normal(kv, (DIM, DIM), dtype=jnp.float32) * scale
        Wo = jax.random.normal(ko, (DIM, DIM), dtype=jnp.float32) * scale
        return {'x': x, 'Wq': Wq, 'Wk': Wk, 'Wv': Wv, 'Wo': Wo}
    _L0_attn_in = _L0_attn_setup()

    def _L0_ffn_setup():
        import jax, jax.numpy as jnp
        import numpy as np
        B, S, H = (2, 256, 128)
        E, F, K = (64, 64, 8)
        G, TG = (8, 4)
        SCALE = 2.5
        F_SH = 64

        def _gate(x, gate_w, gate_bias):
            scores = jax.nn.sigmoid(x @ gate_w.T)
            sc = scores + gate_bias[None, :]
            T = x.shape[0]
            group_scores = jax.lax.top_k(sc.reshape(T, G, E // G), 2)[0].sum(-1)
            _, gidx = jax.lax.top_k(group_scores, TG)
            gmask = jnp.zeros((T, G), sc.dtype).at[jnp.arange(T)[:, None], gidx].set(1.0)
            smask = jnp.repeat(gmask, E // G, axis=1)
            masked = jnp.where(smask > 0, sc, -jnp.inf)
            _, tidx = jax.lax.top_k(masked, K)
            tw = jnp.take_along_axis(scores, tidx, axis=1)
            tw = tw / (tw.sum(-1, keepdims=True) + 1e-20)
            return (tidx, tw * SCALE)
        key = jax.random.key(seed)
        ks = jax.random.split(key, 9)

        def w(k, shape, fan_in):
            return jax.random.normal(k, shape, jnp.float32) / np.float32(np.sqrt(fan_in))
        return {'hidden_states': jax.random.normal(ks[0], (B, S, H), jnp.float32), 'gate_w': w(ks[1], (E, H), H), 'gate_bias': jax.random.normal(ks[2], (E,), jnp.float32) * 0.01, 'We_gate': w(ks[3], (E, H, F), H), 'We_up': w(ks[4], (E, H, F), H), 'We_down': w(ks[5], (E, F, H), F), 'Ws_gate': w(ks[6], (H, F_SH), H), 'Ws_up': w(ks[7], (H, F_SH), H), 'Ws_down': w(ks[8], (F_SH, H), F_SH)}
    _L0_ffn_in = _L0_ffn_setup()
    _d = {'L0_attn_x': _L0_attn_in['x'], 'L0_attn_Wq': _L0_attn_in['Wq'], 'L0_attn_Wk': _L0_attn_in['Wk'], 'L0_attn_Wv': _L0_attn_in['Wv'], 'L0_attn_Wo': _L0_attn_in['Wo'], 'L0_ffn_gate_w': _L0_ffn_in['gate_w'], 'L0_ffn_gate_bias': _L0_ffn_in['gate_bias'], 'L0_ffn_We_gate': _L0_ffn_in['We_gate'], 'L0_ffn_We_up': _L0_ffn_in['We_up'], 'L0_ffn_We_down': _L0_ffn_in['We_down'], 'L0_ffn_Ws_gate': _L0_ffn_in['Ws_gate'], 'L0_ffn_Ws_up': _L0_ffn_in['Ws_up'], 'L0_ffn_Ws_down': _L0_ffn_in['Ws_down']}
    _x0 = _d['L0_attn_x']
    _d['L0_attn_x'] = jax.random.normal(jax.random.fold_in(jax.random.key(seed), 1), (1, 2048, 128), dtype=_x0.dtype)
    del _x0
    return _d

def reference(L0_attn_x, L0_attn_Wq, L0_attn_Wk, L0_attn_Wv, L0_attn_Wo, L0_ffn_gate_w, L0_ffn_gate_bias, L0_ffn_We_gate, L0_ffn_We_up, L0_ffn_We_down, L0_ffn_Ws_gate, L0_ffn_Ws_up, L0_ffn_Ws_down):

    def _L0_attn_ref(x, Wq, Wk, Wv, Wo):
        import math
        import jax, jax.numpy as jnp
        import numpy as np
        DIM = 128
        N_HEADS = 16
        HEAD_DIM = DIM // N_HEADS
        MAX_SEQ_LEN = 512
        ROPE_BASE = 10000.0

        def _rope_tables(seq_len):
            inv_freq = 1.0 / ROPE_BASE ** (jnp.arange(0, HEAD_DIM, 2, dtype=jnp.float32) / HEAD_DIM)
            t = jnp.arange(seq_len, dtype=jnp.float32)
            freqs = jnp.outer(t, inv_freq)
            return (jnp.cos(freqs), jnp.sin(freqs))

        def _rotate_half(x):
            x1 = x[..., 0::2]
            x2 = x[..., 1::2]
            return jnp.stack([-x2, x1], axis=-1).reshape(x.shape)

        def _apply_rope(xq, xk, cos, sin):
            cos = jnp.repeat(cos, 2, axis=-1)[None, None]
            sin = jnp.repeat(sin, 2, axis=-1)[None, None]
            xq_out = xq * cos + _rotate_half(xq) * sin
            xk_out = xk * cos + _rotate_half(xk) * sin
            return (xq_out, xk_out)
        B, S, _ = x.shape
        q = (x @ Wq.T).reshape(B, S, N_HEADS, HEAD_DIM).transpose(0, 2, 1, 3)
        k = (x @ Wk.T).reshape(B, S, N_HEADS, HEAD_DIM).transpose(0, 2, 1, 3)
        v = (x @ Wv.T).reshape(B, S, N_HEADS, HEAD_DIM).transpose(0, 2, 1, 3)
        cos, sin = _rope_tables(S)
        q, k = _apply_rope(q, k, cos, sin)
        scores = jnp.einsum('bhqd,bhkd->bhqk', q, k) / math.sqrt(HEAD_DIM)
        mask = jnp.triu(jnp.full((S, S), -jnp.inf, dtype=scores.dtype), k=1)
        scores = scores + mask[None, None]
        probs = jax.nn.softmax(scores, axis=-1)
        out = jnp.einsum('bhqk,bhkd->bhqd', probs, v)
        out = out.transpose(0, 2, 1, 3).reshape(B, S, DIM)
        return out @ Wo.T

    def _L0_ffn_ref(hidden_states, gate_w, gate_bias, We_gate, We_up, We_down, Ws_gate, Ws_up, Ws_down):
        import jax, jax.numpy as jnp
        import numpy as np
        B, S, H = (2, 256, 128)
        E, F, K = (64, 64, 8)
        G, TG = (8, 4)
        SCALE = 2.5
        F_SH = 64

        def _gate(x, gate_w, gate_bias):
            scores = jax.nn.sigmoid(x @ gate_w.T)
            sc = scores + gate_bias[None, :]
            T = x.shape[0]
            group_scores = jax.lax.top_k(sc.reshape(T, G, E // G), 2)[0].sum(-1)
            _, gidx = jax.lax.top_k(group_scores, TG)
            gmask = jnp.zeros((T, G), sc.dtype).at[jnp.arange(T)[:, None], gidx].set(1.0)
            smask = jnp.repeat(gmask, E // G, axis=1)
            masked = jnp.where(smask > 0, sc, -jnp.inf)
            _, tidx = jax.lax.top_k(masked, K)
            tw = jnp.take_along_axis(scores, tidx, axis=1)
            tw = tw / (tw.sum(-1, keepdims=True) + 1e-20)
            return (tidx, tw * SCALE)
        b, s, h = hidden_states.shape
        x = hidden_states.reshape(-1, h).astype(jnp.float32)
        tidx, tw = _gate(x, gate_w, gate_bias)
        T = x.shape[0]
        w_dense = jnp.zeros((T, E), tw.dtype).at[jnp.arange(T)[:, None], tidx].add(tw)

        def body(acc, ws):
            wg, wu, wdn, cw = ws
            hmid = jax.nn.silu(x @ wg) * (x @ wu)
            return (acc + cw[:, None] * (hmid @ wdn), None)
        y, _ = jax.lax.scan(body, jnp.zeros_like(x), (We_gate, We_up, We_down, w_dense.T))
        y = y.reshape(b, s, h)
        shared = jax.nn.silu(hidden_states @ Ws_gate) * (hidden_states @ Ws_up) @ Ws_down
        return y + shared
    x = L0_attn_x
    xn = _layernorm(x, axis=-1)
    x = x + _L0_attn_ref(xn, L0_attn_Wq, L0_attn_Wk, L0_attn_Wv, L0_attn_Wo) + _L0_ffn_ref(xn, L0_ffn_gate_w, L0_ffn_gate_bias, L0_ffn_We_gate, L0_ffn_We_up, L0_ffn_We_down, L0_ffn_Ws_gate, L0_ffn_Ws_up, L0_ffn_Ws_down)
    return x

_drawn_inputs = setup_inputs


def setup_inputs(seed=0):
    import zlib

    import numpy as np

    out = dict(_drawn_inputs(seed))
    spreads = {}
    factors = {'L0_attn_Wq': 8.0, 'L0_attn_Wk': 8.0, 'L0_attn_Wv': 8.0, 'L0_attn_Wo': 8.0}
    for name, (base, spread) in spreads.items():
        noise = np.random.default_rng([zlib.crc32(name.encode()), seed]).standard_normal(out[name].shape)
        drawn = base * np.exp(spread * noise) if base else spread * noise
        out[name] = jnp.asarray(drawn.astype(out[name].dtype))
    for name, factor in factors.items():
        out[name] = (out[name] * factor).astype(out[name].dtype)
    return out
```

```python
from contextlib import ExitStack

import numpy as np

import concourse.bass as bass
from concourse import mybir

ALU = mybir.AluOpType
ACT = mybir.ActivationFunctionType
AX = mybir.AxisListType
F32 = mybir.dt.float32
BF16 = mybir.dt.bfloat16
I32 = mybir.dt.int32

P = 128
T = 2048
NT = T // P
H, DH = 16, 8
HG = 4
NG = H // HG
CH = 512
NC = T // CH
E, F, K = 64, 64, 8
G, TG = 8, 4
ROUTE_SCALE = 2.5
EPS = 1e-5
SLOT_TILES = 192
XT_TILES = SLOT_TILES + NT
FB = 4
FSTEPS = XT_TILES // FB
UNROLL = 4
HALF = 64
PRODUCTS = 6
SHIFT_ROW = PRODUCTS * DH
Q_PART = [0, 0, 1, 1, 0, 2]
K_PART = [0, 1, 0, 1, 2, 0]
NEG = -1e30
LOW, MARK = -3e38, 3.3e38

UNITS = [HG * (2 * c + 2) for c in range(NC)]
UNITS_G = sum(UNITS)
BLOCKS = [HG * HG * (c + 1) for c in range(NC)]
BLOCKS_G = sum(BLOCKS)
LEAD = 76
CONST = ["ident", "rot", "ltri", "mask_q", "mask_k", "tri", "kid"]
CONST_W = [P, P, P, P, P, G * G, 2]
CONST_AT = {n: sum(CONST_W[:i]) for i, n in enumerate(CONST)}


def unit_of(u):
    c = 0
    while u >= UNITS[c]:
        u -= UNITS[c]
        c += 1
    pair, hh = u // HG, u % HG
    tiles = [2 * pair, 2 * pair + 1]
    return c, hh, [(j, max(0, (j - 4 * c)) * P) for j in tiles]


def block_of(k):
    c = 0
    while k >= BLOCKS[c]:
        k -= BLOCKS[c]
        c += 1
    kb = k % (c + 1)
    hh = k // (c + 1) % HG
    r = k // (c + 1) // HG
    return c, hh, r, kb, (CH if kb < c else P * (r + 1))


def unit_columns(u):
    c, _, tiles = unit_of(u)
    w = [CH - q0 for _, q0 in tiles]
    return [(0, w[0]), (CH if w[0] + w[1] > CH else w[0], w[1])]


FIRST_QUAD = [0]
for n in UNITS:
    FIRST_QUAD.append(FIRST_QUAD[-1] + n // HG)
QUADS_G = FIRST_QUAD[-1]
BLOCK_END = [sum(BLOCKS[:c + 1]) for c in range(NC)]


def plan(last, combine):
    blocks = list(range(LEAD, BLOCKS_G)) + ([] if last else list(range(BLOCKS_G, BLOCKS_G + LEAD)))
    steps, pending = [], []
    nb = 0

    def block():
        nonlocal nb
        if nb < len(blocks):
            k = blocks[nb]
            steps.append(("block", k))
            nb += 1
            if k % BLOCKS_G + 1 in BLOCK_END:
                n = k // BLOCKS_G * NC + BLOCK_END.index(k % BLOCKS_G + 1)
                steps.append(("max_done", n))
                pending.append([3, ("shift", n)])

    def tick():
        for p in pending:
            p[0] -= 1
        while pending and pending[0][0] <= 0:
            steps.append(pending.pop(0)[1])

    def quad(v):
        steps.append(("pv", v))
        for c in range(NC):
            if v == FIRST_QUAD[c + 1] - 1:
                steps.append(("o_copy", c))
                pending.append([2, ("norm", c)])
                if last:
                    pending.append([4, ("project", c)])
                    pending.append([6, ("emit", c)])

    tiles = list(combine)
    for u in range(UNITS_G):
        steps.append(("unit", u))
        tick()
        block()
        if u % HG == 1 and u > HG:
            quad(u // HG - 1)
        block()
        if tiles and (u + 1) * len(combine) >= UNITS_G * 0.97 * (len(combine) - len(tiles) + 1):
            steps.append(("combine", tiles.pop(0)))
    while tiles:
        steps.append(("combine", tiles.pop(0)))
    while nb < len(blocks) - 2:
        block()
    quad(QUADS_G - 1)
    while nb < len(blocks):
        block()
    while pending:
        tick()
    return steps


def prologue_plan():
    steps, pending = [], []
    for k in range(LEAD):
        steps.append(("block", k))
        for p in pending:
            p[0] -= 1
        while pending and pending[0][0] <= 0:
            steps.append(pending.pop(0)[1])
        if k + 1 in BLOCK_END:
            n = BLOCK_END.index(k + 1)
            steps.append(("max_done", n))
            pending.append([4, ("shift", n)])
    return steps + [p[1] for p in pending]


def wait(eng, semaphore, value):
    if not (isinstance(value, int) and value <= 0):
        eng.wait_ge(semaphore, value)


def build(nc, x, wq, wk, wv, wo, gate_w, gate_bias, we_gate, we_up, we_down, ws_gate, ws_up, ws_down,
          consts, cosT, sinT, out):
    x_v = x.rearrange("b (i p) d -> p (b i) d", p=P)
    out_v = out.rearrange("b (i p) d -> p (b i) d", p=P)
    q_rows = nc.dram_tensor("q_rows", (H, HALF, T), BF16, kind="Internal").ap()
    k_rows = nc.dram_tensor("k_rows", (H, HALF, T), BF16, kind="Internal").ap()
    x_slots = nc.dram_tensor("x_slots", (XT_TILES * P, P), F32, kind="Internal").ap()
    y_slots = nc.dram_tensor("y_slots", (XT_TILES * P, P), F32, kind="Internal").ap()
    owner_d = nc.dram_tensor("owner_d", (2 * P,), I32, kind="Internal").ap()

    nc.disable_value_cache = True
    with ExitStack() as ctx:
        def sb(name, shape, dt=F32):
            return ctx.enter_context(nc.sbuf_tensor(name, shape, dt))

        def sem(name):
            return ctx.enter_context(nc.semaphore(name))

        ps = ctx.enter_context(nc.psum_tensor("ps", [P, 8, 512], F32))
        psf = ps[:, :, :].rearrange("p b n -> p (b n)")
        S_BANK, M_BANK, O_BANK, X_BANK = 0, 4, 6, 7

        acc = sb("acc", [P, NT, P])
        xn = sb("xn", [P, NT, P])
        cst = sb("cst", [P, sum(CONST_W)])
        identb, maskqb, maskkb, ltrib, onesb = (sb(n, [P, P], BF16) for n in (
            "identb", "maskqb", "maskkb", "ltrib", "onesb"))
        epsc = sb("epsc", [P, 1])
        woT = sb("woT", [P, P])
        qs = sb("qs", [P, 2 * HG * T], BF16)
        ks = sb("ks", [P, 2 * HG // 2 * T], BF16)
        v_all = sb("v_all", [P, NT, P])
        v_g = sb("v_g", [P, NT, HG, 32])
        probs = sb("probs", [P, 8, 1024])
        attn = sb("attn", [P, NT, P])
        w_gu = sb("w_gu", [P, (E + 1) * 2 * F])
        arena = sb("arena", [P, (E + 1) * P])
        w_dn = arena[0:F, :]
        pos_w = sb("pos_w", [P, NT, K])
        idx = sb("idx", [P, NT, K], I32)
        owner = sb("owner", [1, XT_TILES], I32)
        own_f = sb("own_f", [P, 2])
        own_i = sb("own_i", [P, 2], I32)
        shared_y = sb("shared_y", [P, 2, P])
        mp = sb("mp", [P, 2, HG * HG, NC])
        nm = sb("nm", [P, HG * HG])
        nmr = sb("nmr", [P, 2, HG * HG])
        nmb = sb("nmb", [P, HG * HG, 3], BF16)
        shiftT = sb("shiftT", [3 * HG, 2, CH], BF16)
        o_sb = sb("o_sb", [P, CH])
        rden = sb("rden", [P, HG * HG])
        zrow = sb("zrow", [P, 512])
        stats = sb("stats", [P, NT, 6])
        mv = sb("mv", [P, NT, 2])
        std = sb("std", [P, 2, NT])

        cos_s, sin_s = arena[:, 0:T], arena[:, T:2 * T]
        xnT = arena[:, 2 * T:3 * T]
        wraw = arena[:, 3 * T:3 * T + 5 * P]
        wT = arena[:, 3 * T + 5 * P:3 * T + 10 * P + E]
        ring = probs[:, :, :].rearrange("p b n -> p (b n)")
        score, biased, running, chosen, slot = (ring[:, 1024 * n:1024 * n + 1024] for n in range(5))
        bias_b = ring[:, 5120:5184]
        gt, eq = ring[:, 5184:6208], ring[:, 6208:7232]
        onehot = ring[:, 7232:7744]
        top2, grank, gkeep = (ring[:, 7744 + P * n:7744 + P * n + P] for n in range(3))
        rope_t = [w_gu[:, 512 * n:512 * n + 512] for n in range(6)]
        part_at = [w_gu[:, 3072:3840], w_gu[:, 3840:4608], ring[:, 5184:5952]]
        parts = [[a[:, 256 * n:256 * n + 256].bitcast(BF16) for n in range(3)] for a in part_at]
        level = [w_gu[:, 4608 + a:4608 + a + n] for a, n in (
            (0, 512), (512, 512), (1024, 256), (1280, 256), (1536, 256), (1792, 256),
            (2048, 128), (2176, 128), (2304, 128), (2432, 128))]
        best = w_gu[:, 7168:7296].rearrange("p (i k) -> p i k", k=K)
        slot8 = w_gu[:, 7296:7424].rearrange("p (i k) -> p i k", k=K)
        chosenb = w_gu[:, 7424:7936].bitcast(BF16)
        glow = w_gu[:, 7936:8064]
        ntile, tend, tbase = (w_gu[:, 8064 + 64 * n:8128 + 64 * n] for n in range(3))
        ntile_i = w_gu[:, 8256:8320].bitcast(I32)
        ones64 = sb("ones64", [P, E])
        wsum = sb("wsum", [P, 2, NT])
        x_in = [ring[:, 512 * n:512 * n + 512] for n in range(UNROLL)]
        x_T = [ring[:, 2048 + 512 * n:2560 + 512 * n] for n in range(2)]
        gated = [ring[:, 3072 + 256 * n:3328 + 256 * n] for n in range(2)]
        h_sb = [ring[:, 3584 + 256 * n:3840 + 256 * n] for n in range(2)]
        h_T = [ring[0:F, 4096 + 512 * n:4608 + 512 * n] for n in range(2)]
        y_sb = [ring[:, 5120 + 512 * n:5632 + 512 * n] for n in range(2)]
        a_T, o_out = w_gu[:, 0:CH], w_gu[:, CH:2 * CH]

        def c_(name):
            return cst[:, CONST_AT[name]:CONST_AT[name] + CONST_W[CONST.index(name)]]

        s_x, s_c, s_w, s_cs, s_bias, s_rows = (sem(n) for n in ("s_x", "s_c", "s_w", "s_cs", "s_bias", "s_rows"))
        s_zset, s_zfill, s_cb, s_qzero, s_vset = (sem(n) for n in ("s_zset", "s_zfill", "s_cb", "s_qzero", "s_vset"))
        s_var, s_std, s_xn, s_xt, s_xtc, s_wt, s_wtc = (sem(n) for n in (
            "s_var", "s_std", "s_xn", "s_xt", "s_xtc", "s_wt", "s_wtc"))
        s_lg, s_sig, s_chosen, s_rank, s_idx, s_own = (sem(n) for n in (
            "s_lg", "s_sig", "s_chosen", "s_rank", "s_idx", "s_own"))
        s_ownd, s_ownr, s_disp, s_shx = (sem(n) for n in ("s_ownd", "s_ownr", "s_disp", "s_shx"))
        s_rp, s_rq, s_rope, s_hi, s_r1, s_mid, s_part = (sem(n) for n in (
            "s_rp", "s_rq", "s_rope", "s_hi", "s_r1", "s_mid", "s_part"))
        s_prt = [sem(f"s_prt{b}") for b in range(3)]
        s_v, s_vc, s_ready = sem("s_v"), sem("s_vc"), sem("s_ready")
        s_grp, s_wgu, s_wdn = sem("s_grp"), sem("s_wgu"), sem("s_wdn")
        s_m, s_red, s_nmb, s_nmt = (sem(n) for n in ("s_m", "s_red", "s_nmb", "s_nmt"))
        s_shr = [sem(f"s_shr{b}") for b in range(2)]
        s_sc, s_exp, s_pv, s_vg, s_ocp, s_ot, s_xfree = (sem(n) for n in (
            "s_sc", "s_exp", "s_pv", "s_vg", "s_ocp", "s_ot", "s_xfree"))
        s_fin = [sem(f"s_fin{b}") for b in range(UNROLL)]
        s_fout = [sem(f"s_fout{b}") for b in range(2)]
        s_fxt, s_fxc, s_fgu, s_fe, s_fh, s_fht, s_fhc, s_fy, s_fyc = (sem(n) for n in (
            "s_fxt", "s_fxc", "s_fgu", "s_fe", "s_fh", "s_fht", "s_fhc", "s_fy", "s_fyc"))
        s_gat, s_shy = ([sem(f"{n}{b}") for b in range(2)] for n in ("s_gat", "s_shy"))
        s_comb, s_pr, s_out = (sem(n) for n in ("s_comb", "s_pr", "s_out"))
        s_at = sem("s_at")
        s_dv = sem("s_dv")

        PRO = prologue_plan()
        LOOPED, THIRD, LAST = plan(False, []), plan(False, range(10)), plan(True, range(10, NT))

        def bank_uses(steps, before):
            used = {}
            for s in steps:
                if s[0] in ("shift", "norm", "project", "emit"):
                    used[s] = before + len(used)
            return used

        uses_pro = bank_uses(PRO, 0)
        uses_body = bank_uses(LOOPED, 2)
        uses_last = bank_uses(LAST, 2)

        def bank_use(s, g):
            if g is None:
                return uses_pro[s]
            if isinstance(g, int) and g == NG - 1:
                return uses_last[s] + 8 * g
            return uses_body[s] + 8 * g

        def attention(eng, step, experts):
            for s in PRO:
                step(s, None)
            with eng.Fori(0, 2) as g:
                for s in LOOPED:
                    step(s, eng.snap(g))
            experts()
            for s in THIRD:
                step(s, 2)
            for s in LAST:
                step(s, 3)

        def expert_steps(eng, fstep):
            for b in range(UNROLL):
                fstep(0, b)
            with eng.Fori(1, FSTEPS // UNROLL) as m:
                for b in range(UNROLL):
                    fstep(m, b)
            for b in range(3):
                fstep(FSTEPS // UNROLL, b)

        def back(m, b, d):
            km, kb = m + (b - d) // UNROLL, (b - d) % UNROLL
            k = UNROLL * km + kb
            if isinstance(k, int) and not 0 <= k < FSTEPS:
                return None
            return k, km, kb

        block = ctx.enter_context(nc.Block())

        @block.sync
        def _(sp):
            sp.dma_start(acc[:, :, :], x_v).then_inc(s_x, 16)
            sp.dma_start(cst[:, :], consts).then_inc(s_c, 16)
            for n, w in enumerate((wq, wk, wv, wo)):
                sp.dma_start(wraw[:, n * P:n * P + P], w).then_inc(s_w, 16)
            sp.dma_start(wraw[0:E, 4 * P:5 * P], gate_w).then_inc(s_w, 16)
            sp.dma_start(bias_b, gate_bias.rearrange("(a e) -> a e", a=1).broadcast_to([P, E])).then_inc(s_bias, 16)
            sp.dma_start(cos_s, cosT).then_inc(s_cs, 16)
            sp.dma_start(sin_s, sinT).then_inc(s_cs, 16)
            sp.wait_ge(s_zset, 2)
            sp.dma_start(x_slots[0:SLOT_TILES * P, :].rearrange("(k p r) d -> p k (r d)", p=P, r=4),
                         zrow[:, :].rearrange("p (a n) -> p a n", a=1).broadcast_to([P, SLOT_TILES // 4, 512])
                         ).then_inc(s_zfill, 16)
            zb = zrow[0:H, :].bitcast(BF16).rearrange("p (a n) -> p a n", a=1)
            for rows, r0 in ((q_rows, SHIFT_ROW), (k_rows, SHIFT_ROW + 3)):
                sp.dma_start(rows[:, r0:HALF, :].rearrange("h r (a n) -> h (r a) n", n=1024),
                             zb.broadcast_to([H, 2 * (HALF - r0), 1024])).then_inc(s_rows, 16)
            for r in range(3):
                sp.dma_start(k_rows[:, SHIFT_ROW + r, :].rearrange("h (a n) -> h a n", n=P),
                             onesb[0:H, :].rearrange("p (a n) -> p a n", a=1).broadcast_to([H, T // P, P])
                             ).then_inc(s_rows, 16)
            for n in range(2 * NC):
                z, c = n // NC, n % NC
                sp.wait_ge(s_part, n + 1)
                rows, part = ((k_rows, K_PART), (q_rows, Q_PART))[z]
                for g in range(PRODUCTS):
                    sp.dma_start(rows[:, DH * g:DH * g + DH, CH * c:CH * c + CH], parts[n % 3][part[g]]
                                 ).then_inc(s_prt[n % 3], 16)
            sp.wait_ge(s_rows, 16 * 5)
            for b in range(3):
                sp.wait_ge(s_prt[b], 16 * PRODUCTS * len(range(b, 2 * NC, 3)))
            sp.wait_ge(s_qzero, 2)

            def load_group(group, b):
                for hh in range(HG):
                    r0 = HALF * (hh % 2)
                    for dst, rows, at in ((qs, q_rows, (HG * b + hh) * T), (ks, k_rows, (HG // 2 * b + hh // 2) * T)):
                        src = rows[HG * group + hh] if isinstance(group, int) else rows[
                            bass.ds(HG * group + hh, 1), :, :].rearrange("a r n -> (a r) n")
                        dst = dst[r0:r0 + HALF, at:at + T] if isinstance(group, int) else dst[
                            r0:r0 + HALF, bass.ds(at, T)]
                        sp.dma_start(dst, src).then_inc(s_grp, 16)

            load_group(0, 0)
            load_group(1, 1)
            sp.wait_ge(s_own, 2)
            for col in range(2):
                sp.dma_start(owner_d[P * col:P * col + P].rearrange("(p a) -> p a", a=1), own_i[:, col:col + 1]
                             ).then_inc(s_ownd, 16)
            sp.wait_ge(s_ownd, 32)
            sp.dma_start(owner[0:1, 0:SLOT_TILES], owner_d[0:SLOT_TILES].rearrange("(a k) -> a k", a=1)
                         ).then_inc(s_ownr, 16)
            sp.dma_start(x_slots[SLOT_TILES * P:XT_TILES * P, :].rearrange("(i p) d -> p i d", p=P), xn[:, :, :]
                         ).then_inc(s_shx, 16)
            sp.wait_ge(s_ready, 1)
            w_gu3 = w_gu[:, :].rearrange("p (e f) -> p e f", e=E + 1)
            for w, w_s, at in ((we_gate, ws_gate, 0), (we_up, ws_up, F)):
                sp.dma_start(w_gu3[:, 0:E, at:at + F], w.rearrange("e d f -> d e f")).then_inc(s_wgu, 16)
                sp.dma_start(w_gu3[:, E, at:at + F], w_s).then_inc(s_wgu, 16)
            sp.wait_ge(s_vc, NC)
            sp.dma_start(w_dn[:, 0:E * P].rearrange("f (e d) -> f e d", e=E), we_down.rearrange("e f d -> f e d")
                         ).then_inc(s_wdn, 16)
            sp.dma_start(w_dn[:, E * P:], ws_down).then_inc(s_wdn, 16)

            def step(s, g):
                kind, n = s
                g0 = 0 if g is None else g
                if kind == "shift":
                    c = n % NC
                    b = (g0 + n // NC) % 2
                    sp.wait_ge(s_xfree, bank_use(s, g) + 1)
                    for hh in range(HG):
                        r0 = HALF * (hh % 2) + SHIFT_ROW
                        sp.dma_start(qs[r0:r0 + 3, bass.ds(b * (HG * T) + (hh * T + CH * c), CH)],
                                     shiftT[3 * hh:3 * hh + 3, c % 2, :]).then_inc(s_shr[c % 2], 16)
                elif kind == "emit":
                    sp.wait_ge(s_xfree, bank_use(s, g) + 1)
                    sp.dma_start(out_v[:, 4 * n:4 * n + 4, :], o_out.rearrange("p (r d) -> p r d", r=4)
                                 ).then_inc(s_out, 16)
                elif kind == "combine":
                    wait(sp, s_comb, n - 1)
                    sp.dma_start(shared_y[:, n % 2, :], y_slots[(SLOT_TILES + n) * P:(SLOT_TILES + n + 1) * P, :]
                                 ).then_inc(s_shy[n % 2], 16)

            def load_next(g):
                sp.wait_ge(s_sc, UNITS_G * (g + 1))
                sp.wait_ge(s_grp, 128 * (g + 2))
                load_group(g + 2, g % 2)

            for s in PRO:
                step(s, None)
            with sp.Fori(0, 2) as g:
                for s in LOOPED:
                    step(s, sp.snap(g))
                load_next(g)
            sp.wait_ge(s_disp, 16 * NT * K)
            sp.wait_ge(s_shx, 16)
            sp.wait_ge(s_pv, QUADS_G * 2)

            def fstep(m, b):
                if at := back(m, b, 0):
                    n, _, place = at
                    wait(sp, s_fxt, n - (UNROLL - 1))
                    sp.dma_start(x_in[place].rearrange("p (r d) -> p r d", r=FB),
                                 x_slots[bass.ds(n * (FB * P), FB * P), :].rearrange("(r p) d -> p r d", p=P)
                                 ).then_inc(s_fin[place], 16)

            expert_steps(sp, fstep)
            for b in range(2):
                sp.wait_ge(s_fout[b], 16 * (FSTEPS // 2))
            for steps, g in ((THIRD, 2), (LAST, 3)):
                for s in steps:
                    step(s, g)
            sp.wait_ge(s_out, 16 * NC)

        @block.gpsimd
        def _(pool):
            q3 = qs[:, :].rearrange("p (b m o n) -> p b m o n", b=2, m=HG // 2, o=2)
            for o in range(2):
                r0 = HALF * (1 - o)
                wait(pool, s_qzero, o)
                pool.memset(q3[r0:r0 + HALF, :, :, o, :], 0.0).then_inc(s_qzero, 1)
            pool.wait_ge(s_qzero, 2)
            pool.memset(v_g[:, :, :, DH + 1:], 0.0).then_inc(s_vset, 1)
            pool.memset(v_g[:, :, :, DH:DH + 1], 1.0).then_inc(s_vset, 1)
            pool.wait_ge(s_xn, NT)
            pool.wait_ge(s_idx, 1)
            pool.wait_ge(s_zfill, 16)
            for i in range(NT):
                for j in range(K):
                    pool.indirect_dma_start(x_slots, bass.IndirectOffsetOnAxis(ap=idx[:, i, j:j + 1], axis=0),
                                            xn[:, i, :], None).then_inc(s_disp, 16)
            def fstep(m, b):
                if at := back(m, b, 3):
                    n, _, place = at
                    pool.wait_ge(s_fyc, n + 1)
                    pool.dma_start(y_slots[bass.ds(n * (FB * P), FB * P), :].rearrange("(r p) d -> p r d", p=P),
                                   y_sb[place % 2].rearrange("p (r d) -> p r d", r=FB)
                                   ).then_inc(s_fout[place % 2], 16)

            expert_steps(pool, fstep)
            pool.wait_ge(s_disp, 16 * NT * K)
            pool.wait_ge(s_shx, 16)
            for b in range(2):
                pool.wait_ge(s_fout[b], 16 * (FSTEPS // 2))
            for i in range(NT):
                wait(pool, s_comb, i - 1)
                for j in range(K):
                    pool.indirect_dma_start(xn[:, K * (i % 2) + j, :], None, y_slots,
                                            bass.IndirectOffsetOnAxis(ap=idx[:, i, j:j + 1], axis=0)
                                            ).then_inc(s_gat[i % 2], 16)

        @block.scalar
        def _(act):
            act.wait_ge(s_cb, 5)
            act.wait_ge(s_var, 1)
            nc.scalar.activation(std[:, 0, :], mv[:, :, 1], ACT.Sqrt, bias=epsc[:, 0:1]).then_inc(s_std, 1)
            act.wait_ge(s_wt, 1)
            nc.scalar.copy(wT[:, 0:256], ps[:, 0, 0:256]).then_inc(s_wtc, 1)
            act.wait_ge(s_wt, 2)
            nc.scalar.copy(wT[:, 256:512], ps[:, 1, 0:256]).then_inc(s_wtc, 1)
            act.wait_ge(s_wt, 3)
            nc.scalar.copy(wT[:, 512:704], ps[:, 2, 0:192]).then_inc(s_wtc, 1)
            nc.scalar.copy(woT[:, :], ps[:, 2, 256:384]).then_inc(s_wtc, 1)
            for c in range(NC):
                act.wait_ge(s_xt, c + 1)
                nc.scalar.copy(xnT[:, CH * c:CH * c + CH], ps[:, 3 + c, :]).then_inc(s_xtc, 1)
            for b in range(2):
                act.wait_ge(s_lg, b + 1)
                nc.scalar.activation(score[:, 512 * b:512 * b + 512], ps[:, b, :], ACT.Sigmoid).then_inc(s_sig, 1)
            for c in range(NC):
                act.wait_ge(s_v, c + 1)
                nc.scalar.copy(v_all[:, 4 * c:4 * c + 4, :].rearrange("p i d -> p (i d)"), ps[:, 7 - c % 2, :]
                               ).then_inc(s_vc, 1)
            for n in range(2 * NC + 1):
                if n < 2 * NC:
                    act.wait_ge(s_rope, n + 1)
                    if n >= 3:
                        act.wait_ge(s_prt[n % 3], 16 * PRODUCTS * (n // 3))
                    nc.scalar.copy(parts[n % 3][0], rope_t[2 + n % 2]).then_inc(s_hi, 1)
                if n >= 1:
                    act.wait_ge(s_r1, n)
                    nc.scalar.copy(parts[(n - 1) % 3][1], rope_t[4 + (n - 1) % 2]).then_inc(s_mid, 1)
            act.wait_ge(s_ready, 1)
            act.wait_ge(s_vset, 2)

            def step(s, g):
                kind, n = s
                if kind == "unit":
                    c, hh, tiles = unit_of(n)
                    u = UNITS_G * g + n
                    act.wait_ge(s_sc, u + 1)
                    wait(act, s_pv, QUADS_G * g + max(n // HG - 1, 0))
                    cols = unit_columns(n)
                    w = cols[1][0] + cols[1][1]
                    s0 = 1024 * (n % 2)
                    nc.scalar.activation(probs[:, n % 8, 0:w], psf[:, s0:s0 + w], ACT.Exp,
                                         scale=float(DH) ** -0.5).then_inc(s_exp, 1)
                    if n == 1:
                        src = v_all[:, :, HG * DH * g:HG * DH * (g + 1)] if isinstance(g, int) else v_all[
                            :, :, bass.ds(g * (HG * DH), HG * DH)]
                        nc.scalar.copy(v_g[:, :, :, 0:DH], src.rearrange("p i (h d) -> p i h d", h=HG)
                                       ).then_inc(s_vg, 1)
                elif kind == "o_copy":
                    act.wait_ge(s_pv, QUADS_G * g + FIRST_QUAD[n + 1])
                    wait(act, s_ot, NC * g + n)
                    nc.scalar.copy(o_sb[:, :], ps[:, O_BANK, :]).then_inc(s_ocp, 1)
                elif kind == "project":
                    act.wait_ge(s_at, n + 1)
                    wait(act, s_pr, n)
                    nc.scalar.copy(a_T, ps[:, X_BANK, :]).then_inc(s_xfree, 1)

            def experts():
                def fstep(m, b):
                    if at := back(m, b, 0):
                        n, _, place = at
                        act.wait_ge(s_fxt, n + 1)
                        wait(act, s_fgu, n - 1)
                        nc.scalar.copy(x_T[place % 2], ps[:, place % 2, :]).then_inc(s_fxc, 1)
                    if at := back(m, b, 1):
                        n, _, place = at
                        act.wait_ge(s_fgu, n + 1)
                        wait(act, s_fh, n - 1)
                        gate = ps[:, 2 + place % 2, :].rearrange("p (r f) -> p r f", r=FB)[:, :, 0:F]
                        nc.scalar.activation(gated[place % 2].rearrange("p (r f) -> p r f", r=FB), gate, ACT.Silu
                                             ).then_inc(s_fe, 1)
                    if at := back(m, b, 2):
                        n, _, place = at
                        act.wait_ge(s_fht, n + 1)
                        wait(act, s_fy, n - 1)
                        for o in range(2):
                            nc.scalar.copy(h_T[place % 2][:, 2 * P * o:2 * P * o + 2 * P],
                                           ps[F * o:F * o + F, 4 + place % 2, 0:2 * P]).then_inc(s_fhc, 1)

                expert_steps(act, fstep)
                for b in range(2):
                    act.wait_ge(s_fout[b], 16 * (FSTEPS // 2))

            attention(act, step, experts)

        @block.vector
        def _(dve):
            chain = [0]

            def link(ins):
                chain[0] = chain[0] + 1
                ins.then_inc(s_dv, 1)
                dve.wait_ge(s_dv, chain[0])

            V = nc.vector
            V.memset(zrow[:, :], 0.0).then_inc(s_zset, 1)
            V.memset(onesb[:, :], 1.0).then_inc(s_zset, 1)
            V.memset(epsc[:, :], EPS).then_inc(s_cb, 1)
            V.memset(owner[:, :], E * P).then_inc(s_cb, 1)
            link(V.memset(ones64[:, :], 1.0))
            dve.wait_ge(s_x, 16)
            for i in range(NT):
                last = V.bn_stats(stats[:, i, :], acc[:, i, :])
            link(last)
            for i in range(NT):
                last = V.bn_aggr(mv[:, i, :], stats[:, i, :])
            last.then_inc(s_var, 1)
            dve.wait_ge(s_c, 16)
            for dst, src in ((identb, "ident"), (maskqb, "mask_q"), (maskkb, "mask_k")):
                last = V.tensor_copy(dst[:, :], c_(src))
            last.then_inc(s_cb, 1)
            V.tensor_copy(ltrib[:, :], c_("ltri")).then_inc(s_cb, 1)
            V.memset(nmb[:, :, :], 0.0).then_inc(s_cb, 1)
            dve.wait_ge(s_std, 1)
            link(V.reciprocal(std[:, 1, :], std[:, 0, :]))
            for i in range(NT):
                V.tensor_scalar(xn[:, i, :], acc[:, i, :], mv[:, i, 0:1], std[:, 1, i:i + 1],
                                ALU.subtract, ALU.mult).then_inc(s_xn, 1)

            def ie(a, n=E):
                return a.rearrange("p (i e) -> p i e", e=n)

            dve.wait_ge(s_sig, 2)
            dve.wait_ge(s_bias, 16)
            link(V.tensor_tensor(ie(biased), ie(score), bias_b.rearrange("p (a e) -> p a e", a=1)
                                 .broadcast_to([P, NT, E]), ALU.add))
            hi1, lo1, hi2, t2, u2, lo2, hi3, t3, u3, lo3 = level
            b8, h4, l4 = ie(biased, 8), ie(hi1, 4), ie(lo1, 4)
            V.tensor_tensor(h4, b8[:, :, 0:4], b8[:, :, 4:8], ALU.max)
            link(V.tensor_tensor(l4, b8[:, :, 0:4], b8[:, :, 4:8], ALU.min))
            V.tensor_tensor(ie(t2, 2), h4[:, :, 0:2], h4[:, :, 2:4], ALU.min)
            V.tensor_tensor(ie(u2, 2), l4[:, :, 0:2], l4[:, :, 2:4], ALU.max)
            V.tensor_tensor(ie(hi2, 2), h4[:, :, 0:2], h4[:, :, 2:4], ALU.max)
            link(V.memset(std[:, 0, :], 0.0))
            link(V.tensor_tensor(lo2, t2, u2, ALU.max))
            h2, l2 = ie(hi2, 2), ie(lo2, 2)
            V.tensor_tensor(ie(t3, 1), h2[:, :, 0:1], h2[:, :, 1:2], ALU.min)
            V.tensor_tensor(ie(u3, 1), l2[:, :, 0:1], l2[:, :, 1:2], ALU.max)
            V.tensor_tensor(ie(hi3, 1), h2[:, :, 0:1], h2[:, :, 1:2], ALU.max)
            link(V.memset(std[:, 0, :], 0.0))
            link(V.tensor_tensor(lo3, t3, u3, ALU.max))
            link(V.tensor_tensor(top2, hi3, lo3, ALU.add))
            other = top2.rearrange("p (i a g) -> p i a g", a=1, g=G).broadcast_to([P, NT, G, G])
            own = top2.rearrange("p (i g a) -> p i g a", a=1, g=G).broadcast_to([P, NT, G, G])
            gt4, eq4 = (a.rearrange("p (i g o) -> p i g o", g=G, o=G) for a in (gt, eq))
            V.tensor_tensor(eq4, other, own, ALU.is_equal)
            link(V.tensor_tensor(gt4, other, own, ALU.is_gt))
            link(V.tensor_tensor(ie(eq), ie(eq), c_("tri").rearrange("p (a e) -> p a e", a=1)
                                 .broadcast_to([P, NT, G * G]), ALU.mult))
            link(V.tensor_tensor(gt, gt, eq, ALU.add))
            link(V.tensor_reduce(grank, gt4, AX.X, ALU.add))
            link(V.tensor_scalar(gkeep, grank, float(TG), None, ALU.is_lt))
            V.tensor_scalar(glow, gkeep, -1.0, -LOW, ALU.add, ALU.mult)
            keep8 = gkeep.rearrange("p (g a) -> p g a", a=1).broadcast_to([P, NT * G, 8])
            low8 = glow.rearrange("p (g a) -> p g a", a=1).broadcast_to([P, NT * G, 8])
            link(V.tensor_tensor(ie(running, 8), b8, keep8, ALU.mult))
            link(V.tensor_tensor(ie(running, 8), ie(running, 8), low8, ALU.add))
            for i in range(NT):
                last = V.max(best[:, i, :], ie(running)[:, i, :])
            link(last)
            for i in range(NT):
                last = V.match_replace(ie(chosen)[:, i, :], best[:, i, :], ie(running)[:, i, :], MARK)
            link(last)
            link(V.tensor_scalar(chosen, chosen, 3.2e38, None, ALU.is_ge))
            V.tensor_copy(chosenb, chosen).then_inc(s_chosen, 1)
            dve.wait_ge(s_rank, 3)
            link(V.tensor_scalar(ntile_i, ps[:, 7, 0:E], float(P - 1), None, ALU.add))
            link(V.tensor_scalar(ntile_i, ntile_i, 7, None, ALU.logical_shift_right))
            link(V.tensor_copy(ntile, ntile_i))
            link(V.tensor_tensor_scan(tend, ones64[:, :], ntile, 0.0, ALU.mult, ALU.add))
            link(V.tensor_tensor(tbase, tend, ntile, ALU.subtract))
            link(V.tensor_scalar(tbase, tbase, float(P), 1.0, ALU.mult, ALU.add))
            base16 = tbase.rearrange("p (a e) -> p a e", a=1).broadcast_to([P, NT // 2, E])
            for b in range(2):
                last = V.tensor_tensor(ie(slot)[:, 8 * b:8 * b + 8, :], ps[:, b, :].rearrange("p (i e) -> p i e", e=E),
                                       base16, ALU.add)
            link(last)
            link(V.tensor_tensor(slot, slot, chosen, ALU.mult))
            for i in range(NT):
                last = V.max(slot8[:, i, :], ie(slot)[:, i, :])
            link(last)
            V.tensor_scalar(idx[:, :, :], slot8, -1.0, None, ALU.add).then_inc(s_idx, 1)
            for col in range(2):
                V.tensor_scalar(onehot[:, E * col:E * col + E], tend, c_("kid")[:, col:col + 1], None, ALU.is_le)
            link(V.memset(std[:, 0, :], 0.0))
            link(V.memset(std[:, 0, :], 0.0))
            link(V.tensor_reduce(own_f[:, :], onehot[:, 0:2 * E].rearrange("p (c e) -> p c e", c=2), AX.X, ALU.add))
            link(V.tensor_scalar(own_f[:, :], own_f[:, :], float(E - 1), float(P), ALU.min, ALU.mult))
            V.tensor_copy(own_i[:, :], own_f[:, :]).then_inc(s_own, 2)

            dve.wait_ge(s_cs, 32)
            for n in range(2 * NC + 2):
                if n < 2 * NC:
                    c, b = n % NC, 2 + 2 * (n % 2)
                    dve.wait_ge(s_rp, n + 1)
                    wait(dve, s_rope, n)
                    V.tensor_tensor(rope_t[0], ps[:, b, :], cos_s[:, CH * c:CH * c + CH], ALU.mult)
                    link(V.tensor_tensor(rope_t[1], ps[:, b + 1, :], sin_s[:, CH * c:CH * c + CH], ALU.mult))
                    if n >= 2:
                        dve.wait_ge(s_hi, n - 1)
                        dve.wait_ge(s_r1, n - 1)
                    V.tensor_tensor(rope_t[2 + n % 2], rope_t[0], rope_t[1], ALU.add).then_inc(s_rope, 1)
                if 1 <= n <= 2 * NC:
                    a = n - 1
                    dve.wait_ge(s_hi, n)
                    dve.wait_ge(s_rope, n)
                    if a >= 2:
                        dve.wait_ge(s_mid, a - 1)
                        dve.wait_ge(s_part, a - 1)
                    V.tensor_tensor(rope_t[4 + a % 2], rope_t[2 + a % 2], parts[a % 3][0], ALU.subtract
                                    ).then_inc(s_r1, 1)
                if n >= 2:
                    a = n - 2
                    dve.wait_ge(s_mid, n - 1)
                    dve.wait_ge(s_r1, n - 1)
                    V.tensor_tensor(parts[a % 3][2], rope_t[4 + a % 2], parts[a % 3][1], ALU.subtract
                                    ).then_inc(s_part, 1)

            link(V.tensor_tensor(running, score, chosen, ALU.mult))
            link(V.tensor_reduce(wsum[:, 0, :], ie(running), AX.X, ALU.add))
            link(V.tensor_scalar(wsum[:, 0, :], wsum[:, 0, :], 1e-20, None, ALU.add))
            link(V.reciprocal(wsum[:, 1, :], wsum[:, 0, :]))
            oh3 = onehot.rearrange("p (k e) -> p k e", k=K)
            for i in range(NT):
                link(V.tensor_tensor(oh3, ie(slot)[:, i:i + 1, :].broadcast_to([P, K, E]),
                                     slot8[:, i, :].rearrange("p (k a) -> p k a", a=1).broadcast_to([P, K, E]),
                                     ALU.is_equal))
                link(V.tensor_tensor(oh3, oh3, ie(score)[:, i:i + 1, :].broadcast_to([P, K, E]), ALU.mult))
                link(V.tensor_reduce(pos_w[:, i, :], oh3, AX.X, ALU.add))
            link(V.scalar_tensor_tensor(pos_w[:, :, :], pos_w[:, :, :], ROUTE_SCALE,
                                        wsum[:, 1, :].rearrange("p (i a) -> p i a", a=1).broadcast_to([P, NT, K]),
                                        ALU.mult, ALU.mult))
            V.memset(std[:, 0, :], 0.0).then_inc(s_ready, 1)

            def step(s, g):
                kind, n = s
                g0 = 0 if g is None else g
                if kind == "block":
                    kk = BLOCKS_G * g0 + n
                    c, hh, r, kb, w = block_of(n % BLOCKS_G)
                    dve.wait_ge(s_m, kk + 1)
                    V.tensor_reduce(mp[:, c % 2, HG * r + hh, kb:kb + 1], ps[:, M_BANK + n % 2, 0:w], AX.X, ALU.max
                                    ).then_inc(s_red, 1)
                elif kind == "max_done":
                    c = n % NC
                    dve.wait_ge(s_red, BLOCKS_G * (g0 + n // NC) + BLOCK_END[c])
                    link(V.tensor_reduce(nm[:, :], mp[:, c % 2, :, 0:c + 1], AX.X, ALU.max, negate=True))
                    wait(dve, s_nmt, NC * g0 + n)
                    link(V.tensor_copy(nmb[:, :, 0], nm[:, :]))
                    link(V.tensor_tensor(nmr[:, 0, :], nm[:, :], nmb[:, :, 0], ALU.subtract))
                    link(V.tensor_copy(nmb[:, :, 1], nmr[:, 0, :]))
                    V.tensor_tensor(nmb[:, :, 2], nmr[:, 0, :], nmb[:, :, 1], ALU.subtract).then_inc(s_nmb, 1)
                elif kind == "shift":
                    c = n % NC
                    dve.wait_ge(s_nmt, NC * g0 + n + 1)
                    wait(dve, s_shr[c % 2], 64 * (NC // 2 * g0 + n // 2))
                    V.tensor_copy(shiftT[:, c % 2, :], ps[0:3 * HG, X_BANK, 0:CH // 2].bitcast(BF16)
                                  ).then_inc(s_xfree, 1)
                elif kind == "norm":
                    dve.wait_ge(s_ot, NC * g + n + 1)
                    o4 = ps[:, X_BANK, :].rearrange("p (a m) -> p a m", m=32)
                    link(V.reciprocal(rden[:, :].rearrange("p (a m) -> p a m", m=1), o4[:, :, DH:DH + 1]))
                    a4 = attn[:, 4 * n:4 * n + 4, HG * DH * g:HG * DH * (g + 1)] if isinstance(g, int) else attn[
                        :, 4 * n:4 * n + 4, bass.ds(g * (HG * DH), HG * DH)]
                    V.tensor_tensor(a4.rearrange("p r (h d) -> p r h d", h=HG),
                                    ps[:, X_BANK, :].rearrange("p (r h m) -> p r h m", r=4, h=HG)[:, :, :, 0:DH],
                                    rden[:, :].rearrange("p (r h m) -> p r h m", r=4, m=1).broadcast_to(
                                        [P, 4, HG, DH]), ALU.mult).then_inc(s_xfree, 1)
                elif kind == "combine":
                    dve.wait_ge(s_gat[n % 2], 16 * K * (n // 2 + 1))
                    dve.wait_ge(s_shy[n % 2], 16 * (n // 2 + 1))
                    for j in range(K):
                        link(V.scalar_tensor_tensor(acc[:, n, :], xn[:, K * (n % 2) + j, :], pos_w[:, n, j:j + 1],
                                                    acc[:, n, :], ALU.mult, ALU.add))
                    V.tensor_tensor(acc[:, n, :], acc[:, n, :], shared_y[:, n % 2, :], ALU.add).then_inc(s_comb, 1)
                elif kind == "emit":
                    dve.wait_ge(s_pr, n + 1)
                    dve.wait_ge(s_comb, min(4 * n + 4, NT))
                    wait(dve, s_out, 16 * n)
                    V.tensor_tensor(o_out, ps[:, X_BANK, :], acc[:, 4 * n:4 * n + 4, :].rearrange(
                        "p r d -> p (r d)"), ALU.add).then_inc(s_xfree, 1)

            LINKS = {"max_done": 4, "norm": 1, "combine": K}
            per_group = sum(LINKS.get(s[0], 0) for s in LOOPED)

            def experts():
                def fstep(m, b):
                    if at := back(m, b, 1):
                        n, _, place = at
                        dve.wait_ge(s_fe, n + 1)
                        wait(dve, s_fht, n - 1)
                        up = ps[:, 2 + place % 2, :].rearrange("p (r f) -> p r f", r=FB)[:, :, F:2 * F]
                        V.tensor_tensor(h_sb[place % 2].rearrange("p (r f) -> p r f", r=FB), up,
                                        gated[place % 2].rearrange("p (r f) -> p r f", r=FB), ALU.mult
                                        ).then_inc(s_fh, 1)
                    if at := back(m, b, 3):
                        n, km, place = at
                        dve.wait_ge(s_fy, n + 1)
                        wait(dve, s_fout[place % 2], 16 * (UNROLL // 2 * km + place // 2))
                        V.tensor_copy(y_sb[place % 2], ps[:, 6 + place % 2, :]).then_inc(s_fyc, 1)

                expert_steps(dve, fstep)

            for s in PRO:
                step(s, None)
            before = chain[0]
            with dve.Fori(0, 2) as g:
                chain[0] = before + per_group * g
                for s in LOOPED:
                    step(s, dve.snap(g))
            chain[0] = before + per_group * 2
            experts()
            for steps, g in ((THIRD, 2), (LAST, 3)):
                for s in steps:
                    step(s, g)

        @block.tensor
        def _(pe):
            pe.wait_ge(s_c, 16)
            pe.wait_ge(s_w, 16 * 5)
            ident = c_("ident")
            turned = cst[:, CONST_AT["ident"]:CONST_AT["ident"] + 2 * P]
            for n in range(2):
                pe.matmul(ps[:, n, 0:2 * P], wraw[:, n * P:n * P + P], turned, start=True, stop=True).then_inc(s_wt, 1)
            pe.transpose(ps[:, 2, 0:P], wraw[:, 2 * P:3 * P], ident)
            pe.transpose(ps[:, 2, P:P + E], wraw[0:E, 4 * P:5 * P], ident[0:E, 0:E])
            pe.transpose(ps[:, 2, 2 * P:3 * P], wraw[:, 3 * P:4 * P], ident).then_inc(s_wt, 1)
            for i in range(NT):
                pe.wait_ge(s_xn, i + 1)
                last = pe.transpose(ps[:, 3 + i // 4, P * (i % 4):P * (i % 4) + P], xn[:, i, :], ident)
                if i % 4 == 3:
                    last.then_inc(s_xt, 1)
            pe.wait_ge(s_wtc, 4)
            for i in range(NT):
                pe.wait_ge(s_xtc, i // 4 + 1)
                last = pe.matmul(ps[:, i // 8, E * (i % 8):E * (i % 8) + E], xnT[:, P * i:P * i + P],
                                 wT[:, 5 * P:5 * P + E], start=True, stop=True)
                if i % 8 == 7:
                    last.then_inc(s_lg, 1)
            for c in range(NC):
                if c >= 2:
                    pe.wait_ge(s_vc, c - 1)
                for r in range(4):
                    i = 4 * c + r
                    last = pe.matmul(ps[:, 7 - c % 2, P * r:P * r + P], xnT[:, P * i:P * i + P],
                                     wT[:, 4 * P:5 * P], start=True, stop=True)
                last.then_inc(s_v, 1)

            def rope(n):
                z, c = 2 * P * (1 - n // NC), n % NC
                if n >= 2:
                    pe.wait_ge(s_rope, n - 1)
                b = 2 + 2 * (n % 2)
                pe.matmul(ps[:, b, :], wT[:, z:z + P], xnT[:, CH * c:CH * c + CH], start=True, stop=True)
                pe.matmul(ps[:, b + 1, :], wT[:, z + P:z + 2 * P], xnT[:, CH * c:CH * c + CH], start=True, stop=True
                          ).then_inc(s_rp, 1)

            rope(0)
            rope(1)
            pe.wait_ge(s_chosen, 1)
            pe.wait_ge(s_cb, 5)
            pe.wait_ge(s_zset, 2)
            pe.wait_ge(s_sig, 2)
            pe.wait_ge(s_vc, NC)
            ch3 = chosenb.rearrange("p (i e) -> p i e", e=E)
            for b in range(2):
                i0, i1 = 8 * b, 8 * b + 8
                pe.matmul(ps[:, b, :], ltrib[:, :], chosenb[:, 512 * b:512 * b + 512], start=True, stop=False)
                for j in range(i1 - 1):
                    a = max(i0, j + 1)
                    last = pe.matmul(ps[:, b, E * (a - i0):512].rearrange("p (i e) -> p i e", e=E), onesb[:, :],
                                     ch3[:, j:j + 1, :].broadcast_to([P, i1 - a, E]), start=False, stop=j == i1 - 2)
                last.then_inc(s_rank, 1)
            for i in range(NT):
                last = pe.matmul(ps[:, 7, 0:E], onesb[:, :], ch3[:, i, :], start=i == 0, stop=i == NT - 1)
            last.then_inc(s_rank, 1)
            for n in range(2, 2 * NC):
                rope(n)
            pe.wait_ge(s_ready, 1)

            def step(s, g):
                kind, n = s
                g0 = 0 if g is None else g
                if kind == "block":
                    kk = BLOCKS_G * g0 + n
                    c, hh, r, kb, w = block_of(n % BLOCKS_G)
                    ahead = n // BLOCKS_G
                    b = (g0 + ahead) % 2
                    if n % BLOCKS_G == 0:
                        pe.wait_ge(s_grp, 128 * (g0 + 2))
                    wait(pe, s_red, kk - 1)
                    bank = ps[:, M_BANK + n % 2, :]
                    diag = kb == c
                    last = pe.matmul(bank[:, 0:w], qs[:, bass.ds(b * (HG * T) + (hh * T + CH * c + P * r), P)],
                                     ks[:, bass.ds(b * (HG // 2 * T) + (hh // 2 * T + CH * kb), w)],
                                     start=True, stop=not diag)
                    if diag:
                        last = pe.matmul(bank[:, w - P:w], identb[:, :], maskqb[:, :], start=False, stop=True)
                    last.then_inc(s_m, 1)
                elif kind == "unit":
                    c, hh, tiles = unit_of(n)
                    b = g0 % 2
                    if n == sum(UNITS[:c]):
                        pe.wait_ge(s_shr[c % 2], 64 * (NC // 2 * g0 + c // 2 + 1))
                    wait(pe, s_exp, UNITS_G * g0 + max(n - 1, 0))
                    for (j, q0), (at, w) in zip(tiles, unit_columns(n)):
                        dst = psf[:, 1024 * (n % 2) + at:1024 * (n % 2) + at + w]
                        diag = j >= 4 * c
                        last = pe.matmul(dst, ks[:, bass.ds(b * (HG // 2 * T) + (hh // 2 * T + P * j), P)],
                                         qs[:, bass.ds(b * (HG * T) + (hh * T + CH * c + q0), w)],
                                         start=True, stop=not diag)
                        if diag:
                            last = pe.matmul(dst[:, 0:P], identb[:, :], maskkb[:, :], start=False, stop=True)
                    last.then_inc(s_sc, 1)
                elif kind == "pv":
                    pe.wait_ge(s_exp, UNITS_G * g0 + HG * n + HG)
                    c = unit_of(HG * n)[0]
                    if n == FIRST_QUAD[c]:
                        wait(pe, s_ocp, NC * g0 + c)
                    if n == 0:
                        pe.wait_ge(s_vg, g0 + 1)
                    for t in range(2):
                        for hh in range(HG):
                            u = HG * n + hh
                            j, q0 = unit_of(u)[2][t]
                            at, w = unit_columns(u)[t]
                            last = pe.matmul(ps[32 * hh:32 * hh + 32, O_BANK, q0:CH], v_g[:, j, hh, :],
                                             probs[:, u % 8, at:at + w], start=j == 0, stop=j == 4 * c + 3)
                    last.then_inc(s_pv, 1)
                elif kind == "shift":
                    pe.wait_ge(s_nmb, NC * g0 + n + 1)
                    wait(pe, s_xfree, bank_use(s, g))
                    xb = ps[0:3 * HG, X_BANK, 0:CH // 2].bitcast(BF16)
                    for r in range(4):
                        last = pe.transpose(xb[:, P * r:P * r + P], nmb[:, HG * r:HG * r + HG, :].rearrange(
                            "p h t -> p (h t)"), identb[:, :])
                    last.then_inc(s_nmt, 1)
                elif kind == "norm":
                    pe.wait_ge(s_ocp, NC * g0 + n + 1)
                    wait(pe, s_xfree, bank_use(s, g))
                    for r in range(4):
                        last = pe.transpose(ps[:, X_BANK, P * r:P * r + P], o_sb[:, P * r:P * r + P], ident)
                    last.then_inc(s_ot, 1)
                elif kind == "project":
                    wait(pe, s_xfree, bank_use(s, g))
                    for r in range(4):
                        last = pe.transpose(ps[:, X_BANK, P * r:P * r + P], attn[:, 4 * n + r, :], ident)
                    last.then_inc(s_at, 1)
                elif kind == "emit":
                    wait(pe, s_xfree, bank_use(s, g))
                    for r in range(4):
                        last = pe.matmul(ps[:, X_BANK, P * r:P * r + P], a_T[:, P * r:P * r + P], woT[:, :],
                                         start=True, stop=True)
                    last.then_inc(s_pr, 1)

            def experts():
                pe.wait_ge(s_exp, UNITS_G * 2)
                pe.wait_ge(s_red, BLOCKS_G * 2 + LEAD)
                pe.wait_ge(s_ocp, NC * 2)
                pe.wait_ge(s_xfree, 2 + 8 * 2)
                pe.wait_ge(s_wgu, 16 * 4)
                pe.wait_ge(s_wdn, 16 * 2)
                pe.wait_ge(s_ownr, 16)

                def owners(n):
                    return nc.values_load_multi_w_load_instructions(
                        owner[0:1, bass.ds(n * FB, FB)], engines=[mybir.EngineType.PE], min_val=0, max_val=E * P,
                        skip_runtime_bounds_check_because="VectorE caps the numbers at E")[1]

                def fstep(m, b):
                    if at := back(m, b, 0):
                        n, km, place = at
                        pe.wait_ge(s_fin[place], 16 * (km + 1))
                        wait(pe, s_fxc, n - 1)
                        for r in range(FB):
                            last = pe.transpose(ps[:, place % 2, P * r:P * r + P], x_in[place][:, P * r:P * r + P],
                                                ident)
                        last.then_inc(s_fxt, 1)
                    if at := back(m, b, 1):
                        n, _, place = at
                        pe.wait_ge(s_fxc, n + 1)
                        wait(pe, s_fh, n - 1)
                        for r, e in enumerate(owners(n)):
                            last = pe.matmul(ps[:, 2 + place % 2, P * r:P * r + P], x_T[place % 2][:, P * r:P * r + P],
                                             w_gu[:, bass.ds(e, 2 * F)], start=True, stop=True)
                        last.then_inc(s_fgu, 1)
                    if at := back(m, b, 2):
                        n, _, place = at
                        pe.wait_ge(s_fh, n + 1)
                        wait(pe, s_fhc, 2 * (n - 1))
                        for r in range(FB // 2):
                            last = pe.transpose(ps[:, 4 + place % 2, P * r:P * r + P],
                                                h_sb[place % 2][:, P * r:P * r + P], ident)
                        last.then_inc(s_fht, 1)
                    if at := back(m, b, 3):
                        n, _, place = at
                        pe.wait_ge(s_fhc, 2 * (n + 1))
                        wait(pe, s_fyc, n - 1)
                        for r, e in enumerate(owners(n)):
                            at_r = 2 * (r % 2) + r // 2
                            last = pe.matmul(ps[:, 6 + place % 2, P * r:P * r + P], h_T[place % 2][
                                :, P * at_r:P * at_r + P], w_dn[:, bass.ds(e, P)], start=True, stop=True)
                        last.then_inc(s_fy, 1)

                expert_steps(pe, fstep)
                pe.wait_ge(s_fyc, FSTEPS)

            attention(pe, step, experts)


def tables():
    f = np.float32
    turn = np.zeros((P, P), f)
    for i in range(0, P, 2):
        turn[i + 1, i], turn[i, i + 1] = -1.0, 1.0
    a = np.arange(P)
    part = {
        "ident": np.eye(P, dtype=f),
        "rot": turn,
        "ltri": (a[:, None] < a[None, :]).astype(f),
        "mask_q": np.where(a[None, :] > a[:, None], f(NEG), f(0)),
        "mask_k": np.where(a[None, :] < a[:, None], f(NEG), f(0)),
        "tri": np.broadcast_to((a[None, :G] < a[:G, None]).astype(f).reshape(1, G * G), (P, G * G)),
        "kid": np.stack([a, a + P], 1).astype(f),
    }
    consts = np.ascontiguousarray(np.concatenate([part[n] for n in CONST], 1).astype(f))
    inv = f(1.0) / (f(10000.0) ** (np.arange(0, DH, 2, dtype=f) / f(DH)))
    angle = np.outer(np.arange(T, dtype=f), inv).astype(f)
    rows = np.tile(np.repeat(angle.T, 2, axis=0), (H, 1))
    return consts, np.ascontiguousarray(np.cos(rows)), np.ascontiguousarray(np.sin(rows))


_INS = ['L0_attn_x', 'L0_attn_Wq', 'L0_attn_Wk', 'L0_attn_Wv', 'L0_attn_Wo', 'L0_ffn_gate_w', 'L0_ffn_gate_bias',
        'L0_ffn_We_gate', 'L0_ffn_We_up', 'L0_ffn_We_down', 'L0_ffn_Ws_gate', 'L0_ffn_Ws_up', 'L0_ffn_Ws_down']
_OUTS = [((1, T, P), 'float32')]


def kernel(**inputs):
    import numpy as _np
    import concourse.bacc as _bacc
    from concourse import mybir as _mybir
    from concourse.bass_utils import run_bass_kernel_spmd as _run

    nc = _bacc.Bacc("TRN2", target_bir_lowering=False, num_devices=1)
    arrays, args = {}, []
    given = [(n, _np.ascontiguousarray(inputs[n])) for n in _INS] + list(zip(("consts", "cosT", "sinT"), tables()))
    for name, a in given:
        arrays[f"in_{name}_dram"] = a
        args.append(nc.dram_tensor(f"in_{name}_dram", a.shape, _mybir.dt.from_np(a.dtype), kind="ExternalInput").ap())
    for i, (shape, dtype) in enumerate(_OUTS):
        dt = _mybir.dt.from_np(_np.dtype(dtype))
        args.append(nc.dram_tensor(f"out_{i}_dram", shape, dt, kind="ExternalOutput").ap())
    build(nc, *args)
    r = _run(nc, [arrays], core_ids=[0])
    return r.results[0]["out_0_dram"]
```

```python
from contextlib import ExitStack

import numpy as np

import concourse.bass as bass
from concourse import mybir

ALU = mybir.AluOpType
ACT = mybir.ActivationFunctionType
AX = mybir.AxisListType
F32 = mybir.dt.float32
BF16 = mybir.dt.bfloat16
I32 = mybir.dt.int32

P = 128
T = 2048
NT = T // P
H, DH = 16, 8
HG = 4
NG = H // HG
CH = 512
NC = T // CH
E, F, K = 64, 64, 8
G, TG = 8, 4
ROUTE_SCALE = 2.5
EPS = 1e-5
SLOT_TILES = 192
XT_TILES = SLOT_TILES + NT
GATHERS = 6
FB = 4
FSTEPS = XT_TILES // FB
UNROLL = 4
FIRST = 1
HALF = 64
PRODUCTS = 6
SHIFT_ROW = PRODUCTS * DH
Q_PART = [0, 0, 1, 1, 0, 2]
K_PART = [0, 1, 0, 1, 2, 0]
NEG = -1e30
LOW, MARK = -3e38, 3.3e38

UNITS = [HG * HG * (c + 1) for c in range(NC)]
UNITS_G = sum(UNITS)
BLOCKS = [HG * HG * (c + 1) for c in range(NC)]
BLOCKS_G = sum(BLOCKS)
LAG = 4
HOLD = 4
PROBS = 16
RING = [4, 5, 7]
LEAD = 76
CONST = ["ident", "rot", "ltri", "mask_q", "mask_k", "tri", "kid"]
CONST_W = [P, P, P, P, P, G * G, 2]
CONST_AT = {n: sum(CONST_W[:i]) for i, n in enumerate(CONST)}


def unit_of(u):
    c = 0
    while u >= UNITS[c]:
        u -= UNITS[c]
        c += 1
    j, hh = u // HG, u % HG
    return c, hh, j, max(0, j - 4 * c) * P


def block_of(k):
    c = 0
    while k >= BLOCKS[c]:
        k -= BLOCKS[c]
        c += 1
    kb = k % (c + 1)
    hh = k // (c + 1) % HG
    r = k // (c + 1) // HG
    return c, hh, r, kb, (CH if kb < c else P * (r + 1))


UNIT_END = [sum(UNITS[:c + 1]) for c in range(NC)]
BLOCK_END = [sum(BLOCKS[:c + 1]) for c in range(NC)]


def plan(last, combine=(), span=1.0):
    blocks = list(range(LEAD, BLOCKS_G)) + ([] if last else list(range(BLOCKS_G, BLOCKS_G + LEAD)))
    steps, pending = [], []
    nb = 0

    def block():
        nonlocal nb
        if nb < len(blocks):
            k = blocks[nb]
            steps.append(("block", k))
            nb += 1
            if k % BLOCKS_G + 1 in BLOCK_END:
                n = k // BLOCKS_G * NC + BLOCK_END.index(k % BLOCKS_G + 1)
                steps.append(("max_done", n))
                pending.append([3, ("shift", n)])

    def tick():
        for p in pending:
            p[0] -= 1
        while pending and pending[0][0] <= 0:
            steps.append(pending.pop(0)[1])

    hold = 0
    values = []

    def pv():
        nonlocal hold
        u = values.pop(0)
        steps.append(("pv", u))
        if u + 1 in UNIT_END:
            c = UNIT_END.index(u + 1)
            steps.append(("o_copy", c))
            hold = HOLD
            pending.append([2, ("norm", c)])
            if last:
                pending.append([4, ("project", c)])
                pending.append([6, ("emit", c)])

    parts = [(i, j) for i in combine for j in range(K + 1)]
    for u in range(UNITS_G):
        steps.append(("unit", u))
        tick()
        block()
        if u >= LAG:
            values.append(u - LAG)
        for _ in range(1 + (len(values) > 1)):
            if values and not hold:
                pv()
        if hold:
            hold -= 1
        while parts and (u + 1) * len(combine) * (K + 1) >= UNITS_G * span * (len(combine) * (K + 1) - len(parts) + 1):
            steps.append(("combine", parts.pop(0)))
    assert not parts
    while nb < len(blocks) - 2:
        block()
    values += range(UNITS_G - LAG, UNITS_G)
    while values:
        pv()
    while nb < len(blocks):
        block()
    while pending:
        tick()
    return steps


def prologue_plan():
    steps, pending = [], []
    for k in range(LEAD):
        steps.append(("block", k))
        for p in pending:
            p[0] -= 1
        while pending and pending[0][0] <= 0:
            steps.append(pending.pop(0)[1])
        if k + 1 in BLOCK_END:
            n = BLOCK_END.index(k + 1)
            steps.append(("max_done", n))
            pending.append([4, ("shift", n)])
    return steps + [p[1] for p in pending]


def wait(eng, semaphore, value):
    if not (isinstance(value, int) and value <= 0):
        eng.wait_ge(semaphore, value)


def build(nc, x, wq, wk, wv, wo, gate_w, gate_bias, we_gate, we_up, we_down, ws_gate, ws_up, ws_down,
          consts, cosT, sinT, out):
    x_v = x.rearrange("b (i p) d -> p (b i) d", p=P)
    out_v = out.rearrange("b (i p) d -> p (b i) d", p=P)
    q_rows = nc.dram_tensor("q_rows", (H, HALF, T), BF16, kind="Internal").ap()
    k_rows = nc.dram_tensor("k_rows", (H, HALF, T), BF16, kind="Internal").ap()
    x_slots = nc.dram_tensor("x_slots", (XT_TILES * P, P), F32, kind="Internal").ap()
    y_slots = nc.dram_tensor("y_slots", (XT_TILES * P, P), F32, kind="Internal").ap()
    owner_d = nc.dram_tensor("owner_d", (2 * P,), I32, kind="Internal").ap()

    nc.disable_value_cache = True
    with ExitStack() as ctx:
        def sb(name, shape, dt=F32):
            return ctx.enter_context(nc.sbuf_tensor(name, shape, dt))

        def sem(name):
            return ctx.enter_context(nc.semaphore(name))

        ps = ctx.enter_context(nc.psum_tensor("ps", [P, 8, 512], F32))
        O_BANK = 6

        acc = sb("acc", [P, NT, P])
        xn = sb("xn", [P, NT, P])
        cst = sb("cst", [P, sum(CONST_W)])
        identb, maskqb, maskkb, ltrib, onesb = (sb(n, [P, P], BF16) for n in (
            "identb", "maskqb", "maskkb", "ltrib", "onesb"))
        epsc = sb("epsc", [P, 1])
        woT = sb("woT", [P, P])
        qs = sb("qs", [P, 2 * HG * T], BF16)
        ks = sb("ks", [P, 2 * HG // 2 * T], BF16)
        v_all = sb("v_all", [P, NT, P])
        v_g = sb("v_g", [P, NT, HG, 32])
        probs = sb("probs", [P, PROBS, CH])
        attn = sb("attn", [P, NT, P])
        w_gu = sb("w_gu", [P, (E + 1) * 2 * F])
        arena = sb("arena", [P, (E + 1) * P])
        w_dn = arena[0:F, :]
        pos_w = sb("pos_w", [P, NT, K])
        idx = sb("idx", [P, NT, K], I32)
        owner = sb("owner", [1, XT_TILES], I32)
        own_f = sb("own_f", [P, 2])
        own_i = sb("own_i", [P, 2], I32)
        mp = sb("mp", [P, 2, HG * HG, NC])
        nm = sb("nm", [P, HG * HG])
        nmr = sb("nmr", [P, 2, HG * HG])
        nmb = sb("nmb", [P, HG * HG, 3], BF16)
        shiftT = sb("shiftT", [3 * HG, 2, CH], BF16)
        o_sb = sb("o_sb", [P, CH])
        rden = sb("rden", [P, HG * HG])
        zrow = sb("zrow", [P, 512])
        stats = sb("stats", [P, NT, 6])
        mv = sb("mv", [P, NT, 2])
        std = sb("std", [P, 2, NT])

        cos_s, sin_s = arena[:, 0:T], arena[:, T:2 * T]
        xnT = arena[:, 2 * T:3 * T]
        wraw = arena[:, 3 * T:3 * T + 5 * P]
        wT = arena[:, 3 * T + 5 * P:3 * T + 10 * P + E]
        ring = probs[:, :, :].rearrange("p b n -> p (b n)")
        score, biased, running, chosen, slot = (ring[:, 1024 * n:1024 * n + 1024] for n in range(5))
        bias_b = ring[:, 5120:5184]
        gt, eq = ring[:, 5184:6208], ring[:, 6208:7232]
        onehot = ring[:, 7232:7744]
        top2, grank, gkeep = (ring[:, 7744 + P * n:7744 + P * n + P] for n in range(3))
        rope_t = [w_gu[:, 512 * n:512 * n + 512] for n in range(6)]
        part_at = [w_gu[:, 3072:3840], w_gu[:, 3840:4608], ring[:, 5184:5952]]
        parts = [[a[:, 256 * n:256 * n + 256].bitcast(BF16) for n in range(3)] for a in part_at]
        level = [w_gu[:, 4608 + a:4608 + a + n] for a, n in (
            (0, 512), (512, 512), (1024, 256), (1280, 256), (1536, 256), (1792, 256),
            (2048, 128), (2176, 128), (2304, 128), (2432, 128))]
        best = w_gu[:, 7168:7296].rearrange("p (i k) -> p i k", k=K)
        slot8 = w_gu[:, 7296:7424].rearrange("p (i k) -> p i k", k=K)
        chosenb = w_gu[:, 7424:7936].bitcast(BF16)
        glow = w_gu[:, 7936:8064]
        ntile, tend, tbase = (w_gu[:, 8064 + 64 * n:8128 + 64 * n] for n in range(3))
        ntile_i = w_gu[:, 8256:8320].bitcast(I32)
        ones64 = sb("ones64", [P, E])
        wsum = sb("wsum", [P, 2, NT])
        x_in = [ring[:, 512 * n:512 * n + 512] for n in range(UNROLL)]
        x_T = [ring[:, 2048 + 512 * n:2560 + 512 * n] for n in range(2)]
        gated = [ring[:, 3072 + 256 * n:3328 + 256 * n] for n in range(2)]
        h_sb = [ring[:, 3584 + 256 * n:3840 + 256 * n] for n in range(2)]
        h_T = [ring[0:F, 4096 + 512 * n:4608 + 512 * n] for n in range(2)]
        y_sb = [ring[:, 5120 + 512 * n:5632 + 512 * n] for n in range(2)]
        gathered = [w_gu[:, 2 * CH + K * P * n:2 * CH + K * P * (n + 1)].rearrange("p (j d) -> p j d", j=K)
                    for n in range(GATHERS)]
        a_T, o_out = w_gu[:, 0:CH], w_gu[:, CH:2 * CH]

        def c_(name):
            return cst[:, CONST_AT[name]:CONST_AT[name] + CONST_W[CONST.index(name)]]

        s_x, s_c, s_w, s_cs, s_bias, s_rows = (sem(n) for n in ("s_x", "s_c", "s_w", "s_cs", "s_bias", "s_rows"))
        s_zset, s_zfill, s_cb, s_qzero, s_vset = (sem(n) for n in ("s_zset", "s_zfill", "s_cb", "s_qzero", "s_vset"))
        s_var, s_std, s_xn, s_xt, s_xtc, s_wt, s_wtc = (sem(n) for n in (
            "s_var", "s_std", "s_xn", "s_xt", "s_xtc", "s_wt", "s_wtc"))
        s_lg, s_sig, s_chosen, s_rank, s_idx, s_own = (sem(n) for n in (
            "s_lg", "s_sig", "s_chosen", "s_rank", "s_idx", "s_own"))
        s_ownd, s_ownr, s_disp, s_shx = (sem(n) for n in ("s_ownd", "s_ownr", "s_disp", "s_shx"))
        s_rp, s_rq, s_rope, s_hi, s_r1, s_mid, s_part = (sem(n) for n in (
            "s_rp", "s_rq", "s_rope", "s_hi", "s_r1", "s_mid", "s_part"))
        s_prt = [sem(f"s_prt{b}") for b in range(3)]
        s_v, s_vc, s_ready = sem("s_v"), sem("s_vc"), sem("s_ready")
        s_grp, s_wgu, s_wdn = sem("s_grp"), sem("s_wgu"), sem("s_wdn")
        s_m, s_nmb, s_nmt = (sem(n) for n in ("s_m", "s_nmb", "s_nmt"))
        s_free = [sem(f"s_free{b}") for b in range(len(RING))]
        s_shr = [sem(f"s_shr{b}") for b in range(2)]
        s_sc, s_exp, s_pv, s_vg, s_ocp, s_ot = (sem(n) for n in ("s_sc", "s_exp", "s_pv", "s_vg", "s_ocp", "s_ot"))
        s_fin = [sem(f"s_fin{b}") for b in range(UNROLL)]
        s_fout = [sem(f"s_fout{b}") for b in range(2)]
        s_fxt, s_fxc, s_fgu, s_fe, s_fh, s_fht, s_fhc, s_fy, s_fyc = (sem(n) for n in (
            "s_fxt", "s_fxc", "s_fgu", "s_fe", "s_fh", "s_fht", "s_fhc", "s_fy", "s_fyc"))
        s_gat, s_shy = [sem(f"s_gat{b}") for b in range(GATHERS)], sem("s_shy")
        s_comb, s_pr, s_out = (sem(n) for n in ("s_comb", "s_pr", "s_out"))
        s_at = sem("s_at")
        s_dv = sem("s_dv")

        PRO = prologue_plan()
        LOOPED, THIRD, LAST = plan(False), plan(False, range(9)), plan(True, range(9, NT), 0.7)

        def ring_users(steps):
            return {s: a for a, s in enumerate([s for s in steps if s[0] in (
                "block", "shift", "norm", "project", "emit")])}

        def ring_before(steps):
            n, before = 0, {}
            for s in steps:
                n += s[0] in ("block", "shift", "norm", "project", "emit")
                if s[0] == "max_done":
                    before[s] = n
            return before

        plans = [PRO, LOOPED, THIRD, LAST]
        users, befores = [ring_users(p) for p in plans], [ring_before(p) for p in plans]
        R_PRO, R_G = len(users[0]), len(users[1])
        assert R_PRO % len(RING) == 0 and R_G % len(RING) == 0 and len(users[2]) == R_G

        def of_group(g):
            if g is None:
                return 0, 0
            which = max(1, g)
            return which, R_PRO + R_G * g

        def ring_place(s, g):
            which, base = of_group(g)
            a = users[which][s]
            return RING[a % len(RING)], a // len(RING) + (0 if g is None else R_PRO // len(RING) + R_G // len(RING) * g)

        def ring_sem(bank):
            return s_free[RING.index(bank)]

        def wait_blocks(eng, s, g):
            which, base = of_group(g)
            for a in range(len(RING)):
                n = (befores[which][s] + len(RING) - 1 - a) // len(RING)
                eng.wait_ge(s_free[a], n + (0 if g is None else R_PRO // len(RING) + R_G // len(RING) * g))

        def attention(eng, step, experts):
            for s in PRO:
                step(s, None)
            for g in range(2):
                for s in LOOPED:
                    step(s, g)
            experts()
            for s in THIRD:
                step(s, 2)
            for s in LAST:
                step(s, 3)

        def expert_steps(eng, fstep):
            for m in range(2):
                for b in range(UNROLL):
                    fstep(m, b)
            with eng.Fori(2, FSTEPS // UNROLL) as m:
                for b in range(UNROLL):
                    fstep(m, b)
            for b in range(3):
                fstep(FSTEPS // UNROLL, b)

        def back(m, b, d):
            km, kb = m + (b - d) // UNROLL, (b - d) % UNROLL
            k = UNROLL * km + kb
            if isinstance(k, int) and not 0 <= k < FSTEPS:
                return None
            return k, km, kb

        block = ctx.enter_context(nc.Block())

        @block.sync
        def _(sp):
            sp.dma_start(acc[:, :, :], x_v).then_inc(s_x, 16)
            sp.dma_start(cst[:, :], consts).then_inc(s_c, 16)
            for n, w in enumerate((wq, wk, wv, wo)):
                sp.dma_start(wraw[:, n * P:n * P + P], w).then_inc(s_w, 16)
            sp.dma_start(wraw[0:E, 4 * P:5 * P], gate_w).then_inc(s_w, 16)
            sp.dma_start(bias_b, gate_bias.rearrange("(a e) -> a e", a=1).broadcast_to([P, E])).then_inc(s_bias, 16)
            sp.dma_start(cos_s, cosT).then_inc(s_cs, 16)
            sp.dma_start(sin_s, sinT).then_inc(s_cs, 16)
            sp.wait_ge(s_zset, 2)
            sp.dma_start(x_slots[0:SLOT_TILES * P, :].rearrange("(k p r) d -> p k (r d)", p=P, r=4),
                         zrow[:, :].rearrange("p (a n) -> p a n", a=1).broadcast_to([P, SLOT_TILES // 4, 512])
                         ).then_inc(s_zfill, 16)
            zb = zrow[0:H, :].bitcast(BF16).rearrange("p (a n) -> p a n", a=1)
            for rows, r0 in ((q_rows, SHIFT_ROW), (k_rows, SHIFT_ROW + 3)):
                sp.dma_start(rows[:, r0:HALF, :].rearrange("h r (a n) -> h (r a) n", n=1024),
                             zb.broadcast_to([H, 2 * (HALF - r0), 1024])).then_inc(s_rows, 16)
            for r in range(3):
                sp.dma_start(k_rows[:, SHIFT_ROW + r, :].rearrange("h (a n) -> h a n", n=P),
                             onesb[0:H, :].rearrange("p (a n) -> p a n", a=1).broadcast_to([H, T // P, P])
                             ).then_inc(s_rows, 16)
            for n in range(2 * NC):
                z, c = n // NC, n % NC
                sp.wait_ge(s_part, n + 1)
                rows, part = ((k_rows, K_PART), (q_rows, Q_PART))[z]
                for g in range(PRODUCTS):
                    sp.dma_start(rows[:, DH * g:DH * g + DH, CH * c:CH * c + CH], parts[n % 3][part[g]]
                                 ).then_inc(s_prt[n % 3], 16)
            sp.wait_ge(s_rows, 16 * 5)
            for b in range(3):
                sp.wait_ge(s_prt[b], 16 * PRODUCTS * len(range(b, 2 * NC, 3)))
            sp.wait_ge(s_qzero, 2)

            def load_group(group, b):
                for hh in range(HG):
                    r0 = HALF * (hh % 2)
                    for dst, rows, at in ((qs, q_rows, (HG * b + hh) * T), (ks, k_rows, (HG // 2 * b + hh // 2) * T)):
                        src = rows[HG * group + hh] if isinstance(group, int) else rows[
                            bass.ds(HG * group + hh, 1), :, :].rearrange("a r n -> (a r) n")
                        dst = dst[r0:r0 + HALF, at:at + T] if isinstance(group, int) else dst[
                            r0:r0 + HALF, bass.ds(at, T)]
                        sp.dma_start(dst, src).then_inc(s_grp, 16)

            load_group(0, 0)
            load_group(1, 1)
            sp.wait_ge(s_own, 2)
            for col in range(2):
                sp.dma_start(owner_d[P * col:P * col + P].rearrange("(p a) -> p a", a=1), own_i[:, col:col + 1]
                             ).then_inc(s_ownd, 16)
            sp.wait_ge(s_ownd, 32)
            sp.dma_start(owner[0:1, 0:SLOT_TILES], owner_d[0:SLOT_TILES].rearrange("(a k) -> a k", a=1)
                         ).then_inc(s_ownr, 16)
            sp.dma_start(x_slots[SLOT_TILES * P:XT_TILES * P, :].rearrange("(i p) d -> p i d", p=P), xn[:, :, :]
                         ).then_inc(s_shx, 16)
            sp.wait_ge(s_ready, 1)
            w_gu3 = w_gu[:, :].rearrange("p (e f) -> p e f", e=E + 1)
            for w, w_s, at in ((we_gate, ws_gate, 0), (we_up, ws_up, F)):
                sp.dma_start(w_gu3[:, 0:E, at:at + F], w.rearrange("e d f -> d e f")).then_inc(s_wgu, 16)
                sp.dma_start(w_gu3[:, E, at:at + F], w_s).then_inc(s_wgu, 16)
            sp.wait_ge(s_vc, NC)
            sp.dma_start(w_dn[:, 0:E * P].rearrange("f (e d) -> f e d", e=E), we_down.rearrange("e f d -> f e d")
                         ).then_inc(s_wdn, 16)
            sp.dma_start(w_dn[:, E * P:], ws_down).then_inc(s_wdn, 16)

            def step(s, g):
                kind, n = s
                g0 = 0 if g is None else g
                if kind == "shift":
                    c = n % NC
                    b = (g0 + n // NC) % 2
                    bank, used = ring_place(s, g)
                    sp.wait_ge(ring_sem(bank), used + 1)
                    for hh in range(HG):
                        r0 = HALF * (hh % 2) + SHIFT_ROW
                        sp.dma_start(qs[r0:r0 + 3, bass.ds(b * (HG * T) + (hh * T + CH * c), CH)],
                                     shiftT[3 * hh:3 * hh + 3, c % 2, :]).then_inc(s_shr[c % 2], 16)
                elif kind == "emit":
                    bank, used = ring_place(s, g)
                    sp.wait_ge(ring_sem(bank), used + 1)
                    sp.dma_start(out_v[:, 4 * n:4 * n + 4, :], o_out.rearrange("p (r d) -> p r d", r=4)
                                 ).then_inc(s_out, 16)

            def load_next(g):
                sp.wait_ge(s_sc, UNITS_G * (g + 1))
                sp.wait_ge(s_grp, 128 * (g + 2))
                load_group(g + 2, g % 2)

            for s in PRO:
                step(s, None)
            for g in range(2):
                for s in LOOPED:
                    step(s, g)
                load_next(g)
            sp.wait_ge(s_disp, 16 * NT * K)
            sp.wait_ge(s_shx, 16)
            sp.wait_ge(s_pv, FIRST + UNITS_G * 2)

            def fstep(m, b):
                if at := back(m, b, 0):
                    n, _, place = at
                    wait(sp, s_fxt, n - (UNROLL - 1))
                    sp.dma_start(x_in[place].rearrange("p (r d) -> p r d", r=FB),
                                 x_slots[bass.ds(n * (FB * P), FB * P), :].rearrange("(r p) d -> p r d", p=P)
                                 ).then_inc(s_fin[place], 16)

            expert_steps(sp, fstep)
            for b in range(2):
                sp.wait_ge(s_fout[b], 16 * (FSTEPS // 2))
            sp.dma_start(xn[:, :, :], y_slots[SLOT_TILES * P:XT_TILES * P, :].rearrange("(i p) d -> p i d", p=P)
                         ).then_inc(s_shy, 16)
            for steps, g in ((THIRD, 2), (LAST, 3)):
                for s in steps:
                    step(s, g)
            sp.wait_ge(s_out, 16 * NC)

        @block.gpsimd
        def _(pool):
            q3 = qs[:, :].rearrange("p (b m o n) -> p b m o n", b=2, m=HG // 2, o=2)
            for o in range(2):
                r0 = HALF * (1 - o)
                wait(pool, s_qzero, o)
                pool.memset(q3[r0:r0 + HALF, :, :, o, :], 0.0).then_inc(s_qzero, 1)
            pool.wait_ge(s_qzero, 2)
            pool.memset(v_g[:, :, :, DH + 1:], 0.0).then_inc(s_vset, 1)
            pool.memset(v_g[:, :, :, DH:DH + 1], 1.0).then_inc(s_vset, 1)
            pool.wait_ge(s_xn, NT)
            pool.wait_ge(s_idx, 1)
            pool.wait_ge(s_zfill, 16)
            for i in range(NT):
                for j in range(K):
                    pool.indirect_dma_start(x_slots, bass.IndirectOffsetOnAxis(ap=idx[:, i, j:j + 1], axis=0),
                                            xn[:, i, :], None).then_inc(s_disp, 16)
            def fstep(m, b):
                if at := back(m, b, 3):
                    n, _, place = at
                    pool.wait_ge(s_fyc, n + 1)
                    pool.dma_start(y_slots[bass.ds(n * (FB * P), FB * P), :].rearrange("(r p) d -> p r d", p=P),
                                   y_sb[place % 2].rearrange("p (r d) -> p r d", r=FB)
                                   ).then_inc(s_fout[place % 2], 16)

            expert_steps(pool, fstep)
            pool.wait_ge(s_disp, 16 * NT * K)
            pool.wait_ge(s_shx, 16)
            for b in range(2):
                pool.wait_ge(s_fout[b], 16 * (FSTEPS // 2))
            for i in range(NT):
                wait(pool, s_comb, i - GATHERS + 1)
                for j in range(K):
                    pool.indirect_dma_start(gathered[i % GATHERS][:, j, :], None, y_slots,
                                            bass.IndirectOffsetOnAxis(ap=idx[:, i, j:j + 1], axis=0)
                                            ).then_inc(s_gat[i % GATHERS], 16)

        @block.scalar
        def _(act):
            act.sem_inc(s_exp, FIRST)
            act.sem_inc(s_ocp, FIRST)
            act.wait_ge(s_cb, 5)
            act.wait_ge(s_var, 1)
            nc.scalar.activation(std[:, 0, :], mv[:, :, 1], ACT.Sqrt, bias=epsc[:, 0:1]).then_inc(s_std, 1)
            act.wait_ge(s_wt, 1)
            nc.scalar.copy(wT[:, 0:256], ps[:, 0, 0:256]).then_inc(s_wtc, 1)
            act.wait_ge(s_wt, 2)
            nc.scalar.copy(wT[:, 256:512], ps[:, 1, 0:256]).then_inc(s_wtc, 1)
            act.wait_ge(s_wt, 3)
            nc.scalar.copy(wT[:, 512:704], ps[:, 2, 0:192]).then_inc(s_wtc, 1)
            nc.scalar.copy(woT[:, :], ps[:, 2, 256:384]).then_inc(s_wtc, 1)
            for c in range(NC):
                act.wait_ge(s_xt, c + 1)
                nc.scalar.copy(xnT[:, CH * c:CH * c + CH], ps[:, 3 + c, :]).then_inc(s_xtc, 1)
            for b in range(2):
                act.wait_ge(s_lg, b + 1)
                nc.scalar.activation(score[:, 512 * b:512 * b + 512], ps[:, b, :], ACT.Sigmoid).then_inc(s_sig, 1)
            for c in range(NC):
                act.wait_ge(s_v, c + 1)
                nc.scalar.copy(v_all[:, 4 * c:4 * c + 4, :].rearrange("p i d -> p (i d)"), ps[:, 7 - c % 2, :]
                               ).then_inc(s_vc, 1)
            for n in range(2 * NC + 1):
                if n < 2 * NC:
                    act.wait_ge(s_rope, n + 1)
                    if n >= 3:
                        act.wait_ge(s_prt[n % 3], 16 * PRODUCTS * (n // 3))
                    nc.scalar.copy(parts[n % 3][0], rope_t[2 + n % 2]).then_inc(s_hi, 1)
                if n >= 1:
                    act.wait_ge(s_r1, n)
                    nc.scalar.copy(parts[(n - 1) % 3][1], rope_t[4 + (n - 1) % 2]).then_inc(s_mid, 1)
            act.wait_ge(s_ready, 1)
            act.wait_ge(s_vset, 2)

            def step(s, g):
                kind, n = s
                if kind == "unit":
                    w = CH - unit_of(n)[3]
                    act.wait_ge(s_sc, UNITS_G * g + n + 1)
                    wait(act, s_pv, FIRST + UNITS_G * g + max(n - (PROBS - 1), 0))
                    nc.scalar.activation(probs[:, n % PROBS, 0:w], ps[:, n % 4, 0:w], ACT.Exp,
                                         scale=float(DH) ** -0.5).then_inc(s_exp, 1)
                    if n == 1:
                        src = v_all[:, :, HG * DH * g:HG * DH * (g + 1)] if isinstance(g, int) else v_all[
                            :, :, bass.ds(g * (HG * DH), HG * DH)]
                        nc.scalar.copy(v_g[:, :, :, 0:DH], src.rearrange("p i (h d) -> p i h d", h=HG)
                                       ).then_inc(s_vg, 1)
                elif kind == "o_copy":
                    act.wait_ge(s_pv, FIRST + UNITS_G * g + UNIT_END[n])
                    wait(act, s_ot, FIRST + NC * g + n)
                    nc.scalar.copy(o_sb[:, :], ps[:, O_BANK, :]).then_inc(s_ocp, 1)
                elif kind == "project":
                    act.wait_ge(s_at, n + 1)
                    wait(act, s_pr, n)
                    bank = ring_place(s, g)[0]
                    nc.scalar.copy(a_T, ps[:, bank, :]).then_inc(ring_sem(bank), 1)

            def experts():
                def fstep(m, b):
                    if at := back(m, b, 0):
                        n, _, place = at
                        act.wait_ge(s_fxt, n + 1)
                        wait(act, s_fgu, n - 1)
                        nc.scalar.copy(x_T[place % 2], ps[:, place % 2, :]).then_inc(s_fxc, 1)
                    if at := back(m, b, 1):
                        n, _, place = at
                        act.wait_ge(s_fgu, n + 1)
                        wait(act, s_fh, n - 1)
                        gate = ps[:, 2 + place % 2, :].rearrange("p (r f) -> p r f", r=FB)[:, :, 0:F]
                        nc.scalar.activation(gated[place % 2].rearrange("p (r f) -> p r f", r=FB), gate, ACT.Silu
                                             ).then_inc(s_fe, 1)
                    if at := back(m, b, 2):
                        n, _, place = at
                        act.wait_ge(s_fht, n + 1)
                        wait(act, s_fy, n - 1)
                        for o in range(2):
                            nc.scalar.copy(h_T[place % 2][:, 2 * P * o:2 * P * o + 2 * P],
                                           ps[F * o:F * o + F, 4 + place % 2, 0:2 * P]).then_inc(s_fhc, 1)

                expert_steps(act, fstep)
                for b in range(2):
                    act.wait_ge(s_fout[b], 16 * (FSTEPS // 2))

            attention(act, step, experts)

        @block.vector
        def _(dve):
            chain = [0]

            summed = [0]

            def link(ins, later=False):
                chain[0] = chain[0] + 1
                ins.then_inc(s_dv, 1)
                if not later:
                    dve.wait_ge(s_dv, chain[0])

            V = nc.vector
            V.memset(zrow[:, :], 0.0).then_inc(s_zset, 1)
            V.memset(onesb[:, :], 1.0).then_inc(s_zset, 1)
            V.memset(epsc[:, :], EPS).then_inc(s_cb, 1)
            V.memset(owner[:, :], E * P).then_inc(s_cb, 1)
            link(V.memset(ones64[:, :], 1.0))
            dve.wait_ge(s_x, 16)
            for i in range(NT):
                last = V.bn_stats(stats[:, i, :], acc[:, i, :])
            link(last)
            for i in range(NT):
                last = V.bn_aggr(mv[:, i, :], stats[:, i, :])
            last.then_inc(s_var, 1)
            dve.wait_ge(s_c, 16)
            for dst, src in ((identb, "ident"), (maskqb, "mask_q"), (maskkb, "mask_k")):
                last = V.tensor_copy(dst[:, :], c_(src))
            last.then_inc(s_cb, 1)
            V.tensor_copy(ltrib[:, :], c_("ltri")).then_inc(s_cb, 1)
            V.memset(nmb[:, :, :], 0.0).then_inc(s_cb, 1)
            dve.wait_ge(s_std, 1)
            link(V.reciprocal(std[:, 1, :], std[:, 0, :]))
            for i in range(NT):
                V.tensor_scalar(xn[:, i, :], acc[:, i, :], mv[:, i, 0:1], std[:, 1, i:i + 1],
                                ALU.subtract, ALU.mult).then_inc(s_xn, 1)

            def ie(a, n=E):
                return a.rearrange("p (i e) -> p i e", e=n)

            dve.wait_ge(s_sig, 2)
            dve.wait_ge(s_bias, 16)
            link(V.tensor_tensor(ie(biased), ie(score), bias_b.rearrange("p (a e) -> p a e", a=1)
                                 .broadcast_to([P, NT, E]), ALU.add))
            hi1, lo1, hi2, t2, u2, lo2, hi3, t3, u3, lo3 = level
            b8, h4, l4 = ie(biased, 8), ie(hi1, 4), ie(lo1, 4)
            V.tensor_tensor(h4, b8[:, :, 0:4], b8[:, :, 4:8], ALU.max)
            link(V.tensor_tensor(l4, b8[:, :, 0:4], b8[:, :, 4:8], ALU.min))
            V.tensor_tensor(ie(t2, 2), h4[:, :, 0:2], h4[:, :, 2:4], ALU.min)
            V.tensor_tensor(ie(u2, 2), l4[:, :, 0:2], l4[:, :, 2:4], ALU.max)
            V.tensor_tensor(ie(hi2, 2), h4[:, :, 0:2], h4[:, :, 2:4], ALU.max)
            link(V.memset(std[:, 0, :], 0.0))
            link(V.tensor_tensor(lo2, t2, u2, ALU.max))
            h2, l2 = ie(hi2, 2), ie(lo2, 2)
            V.tensor_tensor(ie(t3, 1), h2[:, :, 0:1], h2[:, :, 1:2], ALU.min)
            V.tensor_tensor(ie(u3, 1), l2[:, :, 0:1], l2[:, :, 1:2], ALU.max)
            V.tensor_tensor(ie(hi3, 1), h2[:, :, 0:1], h2[:, :, 1:2], ALU.max)
            link(V.memset(std[:, 0, :], 0.0))
            link(V.tensor_tensor(lo3, t3, u3, ALU.max))
            link(V.tensor_tensor(top2, hi3, lo3, ALU.add))
            other = top2.rearrange("p (i a g) -> p i a g", a=1, g=G).broadcast_to([P, NT, G, G])
            own = top2.rearrange("p (i g a) -> p i g a", a=1, g=G).broadcast_to([P, NT, G, G])
            gt4, eq4 = (a.rearrange("p (i g o) -> p i g o", g=G, o=G) for a in (gt, eq))
            V.tensor_tensor(eq4, other, own, ALU.is_equal)
            link(V.tensor_tensor(gt4, other, own, ALU.is_gt))
            link(V.tensor_tensor(ie(eq), ie(eq), c_("tri").rearrange("p (a e) -> p a e", a=1)
                                 .broadcast_to([P, NT, G * G]), ALU.mult))
            link(V.tensor_tensor(gt, gt, eq, ALU.add))
            link(V.tensor_reduce(grank, gt4, AX.X, ALU.add))
            link(V.tensor_scalar(gkeep, grank, float(TG), None, ALU.is_lt))
            V.tensor_scalar(glow, gkeep, -1.0, -LOW, ALU.add, ALU.mult)
            keep8 = gkeep.rearrange("p (g a) -> p g a", a=1).broadcast_to([P, NT * G, 8])
            low8 = glow.rearrange("p (g a) -> p g a", a=1).broadcast_to([P, NT * G, 8])
            link(V.tensor_tensor(ie(running, 8), b8, keep8, ALU.mult))
            link(V.tensor_tensor(ie(running, 8), ie(running, 8), low8, ALU.add))
            for i in range(NT):
                last = V.max(best[:, i, :], ie(running)[:, i, :])
            link(last)
            for i in range(NT):
                last = V.match_replace(ie(chosen)[:, i, :], best[:, i, :], ie(running)[:, i, :], MARK)
            link(last)
            link(V.tensor_scalar(chosen, chosen, 3.2e38, None, ALU.is_ge))
            V.tensor_copy(chosenb, chosen).then_inc(s_chosen, 1)
            dve.wait_ge(s_rank, 3)
            link(V.tensor_scalar(ntile_i, ps[:, 7, 0:E], float(P - 1), None, ALU.add))
            link(V.tensor_scalar(ntile_i, ntile_i, 7, None, ALU.logical_shift_right))
            link(V.tensor_copy(ntile, ntile_i))
            link(V.tensor_tensor_scan(tend, ones64[:, :], ntile, 0.0, ALU.mult, ALU.add))
            link(V.tensor_tensor(tbase, tend, ntile, ALU.subtract))
            link(V.tensor_scalar(tbase, tbase, float(P), 1.0, ALU.mult, ALU.add))
            base16 = tbase.rearrange("p (a e) -> p a e", a=1).broadcast_to([P, NT // 2, E])
            for b in range(2):
                last = V.tensor_tensor(ie(slot)[:, 8 * b:8 * b + 8, :], ps[:, b, :].rearrange("p (i e) -> p i e", e=E),
                                       base16, ALU.add)
            link(last)
            link(V.tensor_tensor(slot, slot, chosen, ALU.mult))
            for i in range(NT):
                last = V.max(slot8[:, i, :], ie(slot)[:, i, :])
            link(last)
            V.tensor_scalar(idx[:, :, :], slot8, -1.0, None, ALU.add).then_inc(s_idx, 1)
            for col in range(2):
                V.tensor_scalar(onehot[:, E * col:E * col + E], tend, c_("kid")[:, col:col + 1], None, ALU.is_le)
            link(V.memset(std[:, 0, :], 0.0))
            link(V.memset(std[:, 0, :], 0.0))
            link(V.tensor_reduce(own_f[:, :], onehot[:, 0:2 * E].rearrange("p (c e) -> p c e", c=2), AX.X, ALU.add))
            link(V.tensor_scalar(own_f[:, :], own_f[:, :], float(E - 1), float(P), ALU.min, ALU.mult))
            V.tensor_copy(own_i[:, :], own_f[:, :]).then_inc(s_own, 2)

            dve.wait_ge(s_cs, 32)
            for n in range(2 * NC + 2):
                if n < 2 * NC:
                    c, b = n % NC, 2 + 2 * (n % 2)
                    dve.wait_ge(s_rp, n + 1)
                    wait(dve, s_rope, n)
                    V.tensor_tensor(rope_t[0], ps[:, b, :], cos_s[:, CH * c:CH * c + CH], ALU.mult)
                    link(V.tensor_tensor(rope_t[1], ps[:, b + 1, :], sin_s[:, CH * c:CH * c + CH], ALU.mult))
                    if n >= 2:
                        dve.wait_ge(s_hi, n - 1)
                        dve.wait_ge(s_r1, n - 1)
                    V.tensor_tensor(rope_t[2 + n % 2], rope_t[0], rope_t[1], ALU.add).then_inc(s_rope, 1)
                if 1 <= n <= 2 * NC:
                    a = n - 1
                    dve.wait_ge(s_hi, n)
                    dve.wait_ge(s_rope, n)
                    if a >= 2:
                        dve.wait_ge(s_mid, a - 1)
                        dve.wait_ge(s_part, a - 1)
                    V.tensor_tensor(rope_t[4 + a % 2], rope_t[2 + a % 2], parts[a % 3][0], ALU.subtract
                                    ).then_inc(s_r1, 1)
                if n >= 2:
                    a = n - 2
                    dve.wait_ge(s_mid, n - 1)
                    dve.wait_ge(s_r1, n - 1)
                    V.tensor_tensor(parts[a % 3][2], rope_t[4 + a % 2], parts[a % 3][1], ALU.subtract
                                    ).then_inc(s_part, 1)

            link(V.tensor_tensor(running, score, chosen, ALU.mult))
            link(V.tensor_reduce(wsum[:, 0, :], ie(running), AX.X, ALU.add))
            link(V.tensor_scalar(wsum[:, 0, :], wsum[:, 0, :], 1e-20, None, ALU.add))
            link(V.reciprocal(wsum[:, 1, :], wsum[:, 0, :]))
            oh3 = onehot.rearrange("p (k e) -> p k e", k=K)
            for i in range(NT):
                link(V.tensor_tensor(oh3, ie(slot)[:, i:i + 1, :].broadcast_to([P, K, E]),
                                     slot8[:, i, :].rearrange("p (k a) -> p k a", a=1).broadcast_to([P, K, E]),
                                     ALU.is_equal))
                link(V.tensor_tensor(oh3, oh3, ie(score)[:, i:i + 1, :].broadcast_to([P, K, E]), ALU.mult))
                link(V.tensor_reduce(pos_w[:, i, :], oh3, AX.X, ALU.add))
            link(V.scalar_tensor_tensor(pos_w[:, :, :], pos_w[:, :, :], ROUTE_SCALE,
                                        wsum[:, 1, :].rearrange("p (i a) -> p i a", a=1).broadcast_to([P, NT, K]),
                                        ALU.mult, ALU.mult))
            V.memset(std[:, 0, :], 0.0).then_inc(s_ready, 1)

            def step(s, g):
                kind, n = s
                g0 = 0 if g is None else g
                if kind == "block":
                    kk = BLOCKS_G * g0 + n
                    c, hh, r, kb, w = block_of(n % BLOCKS_G)
                    dve.wait_ge(s_m, kk + 1)
                    bank = ring_place(s, g)[0]
                    V.tensor_reduce(mp[:, c % 2, HG * r + hh, kb:kb + 1], ps[:, bank, 0:w], AX.X, ALU.max
                                    ).then_inc(ring_sem(bank), 1)
                elif kind == "max_done":
                    c = n % NC
                    wait_blocks(dve, s, g)
                    link(V.tensor_reduce(nm[:, :], mp[:, c % 2, :, 0:c + 1], AX.X, ALU.max, negate=True))
                    wait(dve, s_nmt, NC * g0 + n)
                    link(V.tensor_copy(nmb[:, :, 0], nm[:, :]))
                    link(V.tensor_tensor(nmr[:, 0, :], nm[:, :], nmb[:, :, 0], ALU.subtract))
                    link(V.tensor_copy(nmb[:, :, 1], nmr[:, 0, :]))
                    V.tensor_tensor(nmb[:, :, 2], nmr[:, 0, :], nmb[:, :, 1], ALU.subtract).then_inc(s_nmb, 1)
                elif kind == "shift":
                    c = n % NC
                    dve.wait_ge(s_nmt, NC * g0 + n + 1)
                    wait(dve, s_shr[c % 2], 64 * (NC // 2 * g0 + n // 2))
                    bank = ring_place(s, g)[0]
                    V.tensor_copy(shiftT[:, c % 2, :], ps[0:3 * HG, bank, 0:CH // 2].bitcast(BF16)
                                  ).then_inc(ring_sem(bank), 1)
                elif kind == "norm":
                    dve.wait_ge(s_ot, FIRST + NC * g + n + 1)
                    bank = ring_place(s, g)[0]
                    o4 = ps[:, bank, :].rearrange("p (a m) -> p a m", m=32)
                    link(V.reciprocal(rden[:, :].rearrange("p (a m) -> p a m", m=1), o4[:, :, DH:DH + 1]))
                    a4 = attn[:, 4 * n:4 * n + 4, HG * DH * g:HG * DH * (g + 1)] if isinstance(g, int) else attn[
                        :, 4 * n:4 * n + 4, bass.ds(g * (HG * DH), HG * DH)]
                    V.tensor_tensor(a4.rearrange("p r (h d) -> p r h d", h=HG),
                                    ps[:, bank, :].rearrange("p (r h m) -> p r h m", r=4, h=HG)[:, :, :, 0:DH],
                                    rden[:, :].rearrange("p (r h m) -> p r h m", r=4, m=1).broadcast_to(
                                        [P, 4, HG, DH]), ALU.mult).then_inc(ring_sem(bank), 1)
                elif kind == "combine":
                    i, j = n
                    if j == 0:
                        dve.wait_ge(s_shy, 16)
                        link(V.tensor_tensor(acc[:, i, :], acc[:, i, :], xn[:, i, :], ALU.add), later=True)
                    else:
                        if j == 1:
                            dve.wait_ge(s_gat[i % GATHERS], 16 * K * (i // GATHERS + 1))
                        dve.wait_ge(s_dv, summed[0])
                        ins = V.scalar_tensor_tensor(acc[:, i, :], gathered[i % GATHERS][:, j - 1, :],
                                                     pos_w[:, i, j - 1:j], acc[:, i, :], ALU.mult, ALU.add)
                        if j < K:
                            link(ins, later=True)
                        else:
                            ins.then_inc(s_comb, 1)
                    summed[0] = chain[0]
                elif kind == "emit":
                    dve.wait_ge(s_pr, n + 1)
                    dve.wait_ge(s_comb, min(4 * n + 4, NT))
                    wait(dve, s_out, 16 * n)
                    bank = ring_place(s, g)[0]
                    V.tensor_tensor(o_out, ps[:, bank, :], acc[:, 4 * n:4 * n + 4, :].rearrange(
                        "p r d -> p (r d)"), ALU.add).then_inc(ring_sem(bank), 1)

            LINKS = {"max_done": 4, "norm": 1}
            per_group = sum(LINKS.get(s[0], 0) for s in LOOPED)

            def experts():
                def fstep(m, b):
                    if at := back(m, b, 1):
                        n, _, place = at
                        dve.wait_ge(s_fe, n + 1)
                        wait(dve, s_fht, n - 1)
                        up = ps[:, 2 + place % 2, :].rearrange("p (r f) -> p r f", r=FB)[:, :, F:2 * F]
                        V.tensor_tensor(h_sb[place % 2].rearrange("p (r f) -> p r f", r=FB), up,
                                        gated[place % 2].rearrange("p (r f) -> p r f", r=FB), ALU.mult
                                        ).then_inc(s_fh, 1)
                    if at := back(m, b, 3):
                        n, km, place = at
                        dve.wait_ge(s_fy, n + 1)
                        wait(dve, s_fout[place % 2], 16 * (UNROLL // 2 * km + place // 2))
                        V.tensor_copy(y_sb[place % 2], ps[:, 6 + place % 2, :]).then_inc(s_fyc, 1)

                expert_steps(dve, fstep)

            for s in PRO:
                step(s, None)
            before = chain[0]
            for g in range(2):
                chain[0] = before + per_group * g
                for s in LOOPED:
                    step(s, g)
            chain[0] = before + per_group * 2
            experts()
            for steps, g in ((THIRD, 2), (LAST, 3)):
                for s in steps:
                    step(s, g)

        @block.tensor
        def _(pe):
            pe.sem_inc(s_pv, FIRST)
            pe.sem_inc(s_ot, FIRST)
            pe.wait_ge(s_c, 16)
            pe.wait_ge(s_w, 16 * 5)
            ident = c_("ident")
            turned = cst[:, CONST_AT["ident"]:CONST_AT["ident"] + 2 * P]
            for n in range(2):
                pe.matmul(ps[:, n, 0:2 * P], wraw[:, n * P:n * P + P], turned, start=True, stop=True).then_inc(s_wt, 1)
            pe.transpose(ps[:, 2, 0:P], wraw[:, 2 * P:3 * P], ident)
            pe.transpose(ps[:, 2, P:P + E], wraw[0:E, 4 * P:5 * P], ident[0:E, 0:E])
            pe.transpose(ps[:, 2, 2 * P:3 * P], wraw[:, 3 * P:4 * P], ident).then_inc(s_wt, 1)
            for i in range(NT):
                pe.wait_ge(s_xn, i + 1)
                last = pe.transpose(ps[:, 3 + i // 4, P * (i % 4):P * (i % 4) + P], xn[:, i, :], ident)
                if i % 4 == 3:
                    last.then_inc(s_xt, 1)
            pe.wait_ge(s_wtc, 4)
            for i in range(NT):
                pe.wait_ge(s_xtc, i // 4 + 1)
                last = pe.matmul(ps[:, i // 8, E * (i % 8):E * (i % 8) + E], xnT[:, P * i:P * i + P],
                                 wT[:, 5 * P:5 * P + E], start=True, stop=True)
                if i % 8 == 7:
                    last.then_inc(s_lg, 1)
            for c in range(NC):
                if c >= 2:
                    pe.wait_ge(s_vc, c - 1)
                for r in range(4):
                    i = 4 * c + r
                    last = pe.matmul(ps[:, 7 - c % 2, P * r:P * r + P], xnT[:, P * i:P * i + P],
                                     wT[:, 4 * P:5 * P], start=True, stop=True)
                last.then_inc(s_v, 1)

            def rope(n):
                z, c = 2 * P * (1 - n // NC), n % NC
                if n >= 2:
                    pe.wait_ge(s_rope, n - 1)
                b = 2 + 2 * (n % 2)
                pe.matmul(ps[:, b, :], wT[:, z:z + P], xnT[:, CH * c:CH * c + CH], start=True, stop=True)
                pe.matmul(ps[:, b + 1, :], wT[:, z + P:z + 2 * P], xnT[:, CH * c:CH * c + CH], start=True, stop=True
                          ).then_inc(s_rp, 1)

            rope(0)
            rope(1)
            pe.wait_ge(s_chosen, 1)
            pe.wait_ge(s_cb, 5)
            pe.wait_ge(s_zset, 2)
            pe.wait_ge(s_sig, 2)
            pe.wait_ge(s_vc, NC)
            ch3 = chosenb.rearrange("p (i e) -> p i e", e=E)
            for b in range(2):
                i0, i1 = 8 * b, 8 * b + 8
                pe.matmul(ps[:, b, :], ltrib[:, :], chosenb[:, 512 * b:512 * b + 512], start=True, stop=False)
                for j in range(i1 - 1):
                    a = max(i0, j + 1)
                    last = pe.matmul(ps[:, b, E * (a - i0):512].rearrange("p (i e) -> p i e", e=E), onesb[:, :],
                                     ch3[:, j:j + 1, :].broadcast_to([P, i1 - a, E]), start=False, stop=j == i1 - 2)
                last.then_inc(s_rank, 1)
            for i in range(NT):
                last = pe.matmul(ps[:, 7, 0:E], onesb[:, :], ch3[:, i, :], start=i == 0, stop=i == NT - 1)
            last.then_inc(s_rank, 1)
            for n in range(2, 2 * NC):
                rope(n)
            pe.wait_ge(s_ready, 1)

            def step(s, g):
                kind, n = s
                g0 = 0 if g is None else g
                if kind == "block":
                    c, hh, r, kb, w = block_of(n % BLOCKS_G)
                    ahead = n // BLOCKS_G
                    b = (g0 + ahead) % 2
                    if n % BLOCKS_G == 0:
                        pe.wait_ge(s_grp, 128 * (g0 + 2))
                    at, used = ring_place(s, g)
                    wait(pe, ring_sem(at), used)
                    bank = ps[:, at, :]
                    diag = kb == c
                    last = pe.matmul(bank[:, 0:w], qs[:, bass.ds(b * (HG * T) + (hh * T + CH * c + P * r), P)],
                                     ks[:, bass.ds(b * (HG // 2 * T) + (hh // 2 * T + CH * kb), w)],
                                     start=True, stop=not diag)
                    if diag:
                        last = pe.matmul(bank[:, w - P:w], identb[:, :], maskqb[:, :], start=False, stop=True)
                    last.then_inc(s_m, 1)
                elif kind == "unit":
                    c, hh, j, q0 = unit_of(n)
                    b = g0 % 2
                    if n == UNIT_END[c] - UNITS[c]:
                        pe.wait_ge(s_shr[c % 2], 64 * (NC // 2 * g0 + c // 2 + 1))
                    wait(pe, s_exp, FIRST + UNITS_G * g0 + max(n - 3, 0))
                    dst = ps[:, n % 4, 0:CH - q0]
                    diag = j >= 4 * c
                    last = pe.matmul(dst, ks[:, bass.ds(b * (HG // 2 * T) + (hh // 2 * T + P * j), P)],
                                     qs[:, bass.ds(b * (HG * T) + (hh * T + CH * c + q0), CH - q0)],
                                     start=True, stop=not diag)
                    if diag:
                        last = pe.matmul(dst[:, 0:P], identb[:, :], maskkb[:, :], start=False, stop=True)
                    last.then_inc(s_sc, 1)
                elif kind == "pv":
                    pe.wait_ge(s_exp, FIRST + UNITS_G * g0 + n + 1)
                    c, hh, j, q0 = unit_of(n)
                    if n == UNIT_END[c] - UNITS[c]:
                        wait(pe, s_ocp, FIRST + NC * g0 + c)
                    if n == 0:
                        pe.wait_ge(s_vg, g0 + 1)
                    pe.matmul(ps[32 * hh:32 * hh + 32, O_BANK, q0:CH], v_g[:, j, hh, :], probs[:, n % PROBS, 0:CH - q0],
                              start=j == 0, stop=j == 4 * c + 3).then_inc(s_pv, 1)
                elif kind == "shift":
                    pe.wait_ge(s_nmb, NC * g0 + n + 1)
                    bank, used = ring_place(s, g)
                    wait(pe, ring_sem(bank), used)
                    xb = ps[0:3 * HG, bank, 0:CH // 2].bitcast(BF16)
                    for r in range(4):
                        last = pe.transpose(xb[:, P * r:P * r + P], nmb[:, HG * r:HG * r + HG, :].rearrange(
                            "p h t -> p (h t)"), identb[:, :])
                    last.then_inc(s_nmt, 1)
                elif kind == "norm":
                    pe.wait_ge(s_ocp, FIRST + NC * g0 + n + 1)
                    bank, used = ring_place(s, g)
                    wait(pe, ring_sem(bank), used)
                    for r in range(4):
                        last = pe.transpose(ps[:, bank, P * r:P * r + P], o_sb[:, P * r:P * r + P], ident)
                    last.then_inc(s_ot, 1)
                elif kind == "project":
                    bank, used = ring_place(("norm", n), g)
                    pe.wait_ge(ring_sem(bank), used + 1)
                    bank, used = ring_place(s, g)
                    pe.wait_ge(ring_sem(bank), used)
                    for r in range(4):
                        last = pe.transpose(ps[:, bank, P * r:P * r + P], attn[:, 4 * n + r, :], ident)
                    last.then_inc(s_at, 1)
                elif kind == "emit":
                    bank, used = ring_place(("project", n), g)
                    pe.wait_ge(ring_sem(bank), used + 1)
                    bank, used = ring_place(s, g)
                    pe.wait_ge(ring_sem(bank), used)
                    for r in range(4):
                        last = pe.matmul(ps[:, bank, P * r:P * r + P], a_T[:, P * r:P * r + P], woT[:, :],
                                         start=True, stop=True)
                    last.then_inc(s_pr, 1)

            def experts():
                pe.wait_ge(s_exp, FIRST + UNITS_G * 2)
                pe.wait_ge(s_ocp, FIRST + NC * 2)
                for free in s_free:
                    pe.wait_ge(free, (R_PRO + 2 * R_G) // len(RING))
                pe.wait_ge(s_wgu, 16 * 4)
                pe.wait_ge(s_wdn, 16 * 2)
                pe.wait_ge(s_ownr, 16)

                def owners(n):
                    return nc.values_load_multi_w_load_instructions(
                        owner[0:1, bass.ds(n * FB, FB)], engines=[mybir.EngineType.PE], min_val=0, max_val=E * P,
                        skip_runtime_bounds_check_because="VectorE caps the numbers at E")[1]

                def fstep(m, b):
                    if at := back(m, b, 0):
                        n, km, place = at
                        pe.wait_ge(s_fin[place], 16 * (km + 1))
                        wait(pe, s_fxc, n - 1)
                        for r in range(FB):
                            last = pe.transpose(ps[:, place % 2, P * r:P * r + P], x_in[place][:, P * r:P * r + P],
                                                ident)
                        last.then_inc(s_fxt, 1)
                    if at := back(m, b, 1):
                        n, _, place = at
                        pe.wait_ge(s_fxc, n + 1)
                        wait(pe, s_fh, n - 1)
                        for r, e in enumerate(owners(n)):
                            last = pe.matmul(ps[:, 2 + place % 2, P * r:P * r + P], x_T[place % 2][:, P * r:P * r + P],
                                             w_gu[:, bass.ds(e, 2 * F)], start=True, stop=True)
                        last.then_inc(s_fgu, 1)
                    if at := back(m, b, 2):
                        n, _, place = at
                        pe.wait_ge(s_fh, n + 1)
                        wait(pe, s_fhc, 2 * (n - 1))
                        for r in range(FB // 2):
                            last = pe.transpose(ps[:, 4 + place % 2, P * r:P * r + P],
                                                h_sb[place % 2][:, P * r:P * r + P], ident)
                        last.then_inc(s_fht, 1)
                    if at := back(m, b, 3):
                        n, _, place = at
                        pe.wait_ge(s_fhc, 2 * (n + 1))
                        wait(pe, s_fyc, n - 1)
                        for r, e in enumerate(owners(n)):
                            at_r = 2 * (r % 2) + r // 2
                            last = pe.matmul(ps[:, 6 + place % 2, P * r:P * r + P], h_T[place % 2][
                                :, P * at_r:P * at_r + P], w_dn[:, bass.ds(e, P)], start=True, stop=True)
                        last.then_inc(s_fy, 1)

                expert_steps(pe, fstep)
                pe.wait_ge(s_fyc, FSTEPS)

            attention(pe, step, experts)


def tables():
    f = np.float32
    turn = np.zeros((P, P), f)
    for i in range(0, P, 2):
        turn[i + 1, i], turn[i, i + 1] = -1.0, 1.0
    a = np.arange(P)
    part = {
        "ident": np.eye(P, dtype=f),
        "rot": turn,
        "ltri": (a[:, None] < a[None, :]).astype(f),
        "mask_q": np.where(a[None, :] > a[:, None], f(NEG), f(0)),
        "mask_k": np.where(a[None, :] < a[:, None], f(NEG), f(0)),
        "tri": np.broadcast_to((a[None, :G] < a[:G, None]).astype(f).reshape(1, G * G), (P, G * G)),
        "kid": np.stack([a, a + P], 1).astype(f),
    }
    consts = np.ascontiguousarray(np.concatenate([part[n] for n in CONST], 1).astype(f))
    inv = f(1.0) / (f(10000.0) ** (np.arange(0, DH, 2, dtype=f) / f(DH)))
    angle = np.outer(np.arange(T, dtype=f), inv).astype(f)
    rows = np.tile(np.repeat(angle.T, 2, axis=0), (H, 1))
    return consts, np.ascontiguousarray(np.cos(rows)), np.ascontiguousarray(np.sin(rows))


_INS = ['L0_attn_x', 'L0_attn_Wq', 'L0_attn_Wk', 'L0_attn_Wv', 'L0_attn_Wo', 'L0_ffn_gate_w', 'L0_ffn_gate_bias',
        'L0_ffn_We_gate', 'L0_ffn_We_up', 'L0_ffn_We_down', 'L0_ffn_Ws_gate', 'L0_ffn_Ws_up', 'L0_ffn_Ws_down']
_OUTS = [((1, T, P), 'float32')]


def kernel(**inputs):
    import numpy as _np
    import concourse.bacc as _bacc
    from concourse import mybir as _mybir
    from concourse.bass_utils import run_bass_kernel_spmd as _run

    nc = _bacc.Bacc("TRN2", target_bir_lowering=False, num_devices=1)
    arrays, args = {}, []
    given = [(n, _np.ascontiguousarray(inputs[n])) for n in _INS] + list(zip(("consts", "cosT", "sinT"), tables()))
    for name, a in given:
        arrays[f"in_{name}_dram"] = a
        args.append(nc.dram_tensor(f"in_{name}_dram", a.shape, _mybir.dt.from_np(a.dtype), kind="ExternalInput").ap())
    for i, (shape, dtype) in enumerate(_OUTS):
        dt = _mybir.dt.from_np(_np.dtype(dtype))
        args.append(nc.dram_tensor(f"out_{i}_dram", shape, dt, kind="ExternalOutput").ap())
    build(nc, *args)
    r = _run(nc, [arrays], core_ids=[0])
    return r.results[0]["out_0_dram"]
```

```python
from contextlib import ExitStack

import numpy as np

import concourse.bass as bass
from concourse import mybir

ALU = mybir.AluOpType
ACT = mybir.ActivationFunctionType
AX = mybir.AxisListType
F32 = mybir.dt.float32
BF16 = mybir.dt.bfloat16
I32 = mybir.dt.int32

P = 128
T = 2048
NT = T // P
H, DH = 16, 8
HG = 4
NG = H // HG
CH = 512
NC = T // CH
E, F, K = 64, 64, 8
G, TG = 8, 4
ROUTE_SCALE = 2.5
EPS = 1e-5
SLOT_TILES = 192
XT_TILES = SLOT_TILES + NT
ZFILLS, EARLY_ZFILLS = 16, 7
WGAP = 4
WLOADS = 8
GATHERS = 6
FB = 4
FSTEPS = XT_TILES // FB
UNROLL = 4
HALF = 64
PRODUCTS = 6
SHIFT_ROW = PRODUCTS * DH
Q_PART = [0, 0, 1, 1, 0, 2]
K_PART = [0, 1, 0, 1, 2, 0]
NEG = -1e30
LOW, MARK = -3e38, 3.3e38

ORDER = [list(range(NC)), list(range(NC))[::-1]] * (NG // 2)
CHUNKS = [(g, c) for g in range(NG) for c in ORDER[g]]
SIZE = [HG * HG * (c + 1) for _, c in CHUNKS]
END = [sum(SIZE[:m + 1]) for m in range(len(SIZE))]
UNITS_G = END[NC - 1]
QUADS_G = UNITS_G // HG
TILES = [4 * c + r for c in ORDER[-1] for r in range(4)]
MARGIN = 18
SUM_FROM, SUM_TO = 120, 318
MATCH_FROM, WEIGH_FROM = 110, 222
SPLITS, SHIFT_AFTER = 5, 6
PROBS = 16
SCORES, RING, O_BANK = 3, [3, 4, 5, 7], 6
SPARE = FB * (UNROLL - 1)
CONST = ["ident", "rot", "ltri", "mask_q", "mask_k", "tri", "kid"]
CONST_W = [P, P, P, P, P, G * G, 2]
CONST_AT = {n: sum(CONST_W[:i]) for i, n in enumerate(CONST)}


def unit_of(u):
    m = next(m for m in range(len(END)) if u < END[m])
    g, c = CHUNKS[m]
    j, hh = divmod(u - END[m] + SIZE[m], HG)
    return m, g, c, hh, j, max(0, j - 4 * c) * P


def block_of(k):
    m = next(m for m in range(len(END)) if k < END[m])
    g, c = CHUNKS[m]
    r, rest = divmod(k - END[m] + SIZE[m], HG * (c + 1))
    hh, kb = divmod(rest, c + 1)
    return m, g, c, hh, r, kb, (CH if kb < c else P * (r + 1))


def blocks_before(u):
    due = [(END[m] - SIZE[m] - MARGIN, END[m]) for m in range(len(END))]
    best = 0.0
    for ua, ba in due:
        for ub, bb in due:
            if ua <= u <= ub:
                best = max(best, ba if ua == ub else ba + (bb - ba) * (u - ua) / (ub - ua))
    if u >= due[-1][0]:
        best = END[-1]
    return int(best + 0.999)


def plan():
    steps, pending = [], []
    nb, half = 0, UNITS_G * NG // 2
    quads, splits = [], []
    parts = [(i, j) for i in TILES for j in range(K + 1)]

    def block():
        nonlocal nb
        steps.append(("block", nb))
        nb += 1
        if splits:
            split()
        if nb in END:
            splits.extend((END.index(nb), k) for k in range(SPLITS))
            split()
            while splits and nb == END[-1]:
                split()
        tick()

    def split():
        m, k = splits.pop(0)
        steps.append(("max_done", (m, k)))
        if k == SPLITS - 1:
            pending.append([SHIFT_AFTER, ("shift", m)])

    def tick():
        for p in pending:
            p[0] -= 1
        while pending and pending[0][0] <= 0:
            steps.append(pending.pop(0)[1])

    def quad():
        v = quads.pop(0)
        steps.append(("pv", v))
        if HG * (v + 1) in END:
            m = END.index(HG * (v + 1))
            steps.append(("o_copy", m))
            if m % NC == NC - 1 and m + 1 < len(END):
                steps.append(("values", m // NC + 1))
            pending.append([5, ("norm", m)])
            if m // NC == NG - 1:
                pending.append([9, ("project", m)])
                pending.append([13, ("emit", m)])

    while nb < blocks_before(0):
        block()
    steps.append(("values", 0))
    for u in range(END[-1]):
        if u == half:
            while quads:
                quad()
            while pending:
                tick()
            assert not splits
            steps.append(("experts", 0))
        steps.append(("unit", u))
        tick()
        if MATCH_FROM <= u < MATCH_FROM + 5 * NT and (u - MATCH_FROM) % 5 == 0:
            steps.append(("match", (u - MATCH_FROM) // 5))
        if WEIGH_FROM <= u < WEIGH_FROM + 4 * NT and u % 4 == 0:
            steps.append(("weigh", (u - WEIGH_FROM) // 4))
        if u % UNITS_G == 0 and 1 <= u // UNITS_G < NG - 1:
            steps.append(("load", u // UNITS_G + 1))
        while nb < blocks_before(u + 1):
            block()
        if u % HG == HG - 1:
            quads.append(u // HG)
        if len(quads) > 1 and u % HG == 1:
            quad()
        gone = (u - half - SUM_FROM) / (SUM_TO - SUM_FROM)
        while parts and gone * len(TILES) * (K + 1) > len(TILES) * (K + 1) - len(parts):
            steps.append(("combine", parts.pop(0)))
    assert not parts and nb == END[-1]
    while quads:
        quad()
    while pending:
        tick()
    return steps


def wait(eng, semaphore, value):
    if not (isinstance(value, int) and value <= 0):
        eng.wait_ge(semaphore, value)


def build(nc, x, wq, wk, wv, wo, gate_w, gate_bias, we_gate, we_up, we_down, ws_gate, ws_up, ws_down,
          consts, cosT, sinT, out):
    x_v = x.rearrange("b (i p) d -> p (b i) d", p=P)
    out_v = out.rearrange("b (i p) d -> p (b i) d", p=P)
    q_rows = nc.dram_tensor("q_rows", (H, HALF, T), BF16, kind="Internal").ap()
    k_rows = nc.dram_tensor("k_rows", (H, HALF, T), BF16, kind="Internal").ap()
    x_slots = nc.dram_tensor("x_slots", ((XT_TILES + SPARE) * P, P), F32, kind="Internal").ap()
    y_slots = nc.dram_tensor("y_slots", ((XT_TILES + SPARE) * P, P), F32, kind="Internal").ap()
    owner_d = nc.dram_tensor("owner_d", (2 * P,), I32, kind="Internal").ap()

    with ExitStack() as ctx:
        def sb(name, shape, dt=F32):
            return ctx.enter_context(nc.sbuf_tensor(name, shape, dt))

        def sem(name):
            return ctx.enter_context(nc.semaphore(name))

        ps = ctx.enter_context(nc.psum_tensor("ps", [P, 8, 512], F32))

        acc = sb("acc", [P, NT, P])
        xn = sb("xn", [P, NT, P])
        cst = sb("cst", [P, sum(CONST_W)])
        identb, maskqb, maskkb, ltrib, onesb = (sb(n, [P, P], BF16) for n in (
            "identb", "maskqb", "maskkb", "ltrib", "onesb"))
        epsc = sb("epsc", [P, 1])
        woT = sb("woT", [P, P])
        qs = sb("qs", [P, 2 * HG * T], BF16)
        ks = sb("ks", [P, 2 * HG // 2 * T], BF16)
        v_all = sb("v_all", [P, NT, P])
        v_g = sb("v_g", [P, NT, HG, 32])
        probs = sb("probs", [P, PROBS, CH])
        attn = sb("attn", [P, NT, P])
        w_gu = sb("w_gu", [P, (E + 1) * 2 * F])
        arena = sb("arena", [P, (E + 1) * P])
        w_dn = arena[0:F, :]
        pos_w = sb("pos_w", [P, NT, K])
        idx = sb("idx", [P, NT, K], I32)
        owner = sb("owner", [1, XT_TILES + SPARE], I32)
        own_f = sb("own_f", [P, 2])
        own_i = sb("own_i", [P, 2], I32)
        mp = sb("mp", [P, 2, HG * HG, NC])
        nm = sb("nm", [P, HG * HG])
        nmr = sb("nmr", [P, 2, HG * HG])
        nmb = sb("nmb", [P, HG * HG, 3], BF16)
        shiftT = sb("shiftT", [3 * HG, 2, CH], BF16)
        o_sb = sb("o_sb", [P, CH])
        rden = sb("rden", [P, HG * HG])
        zrow = sb("zrow", [P, 512])
        stats = sb("stats", [P, NT, 6])
        mv = sb("mv", [P, NT, 2])
        std = sb("std", [P, 2, NT])

        cos_s, sin_s = arena[:, 0:T], arena[:, T:2 * T]
        xnT = arena[:, 2 * T:3 * T]
        wraw = arena[:, 3 * T:3 * T + 5 * P]
        wT = arena[:, 3 * T + 5 * P:3 * T + 10 * P + E]
        ring = probs[:, :, :].rearrange("p b n -> p (b n)")
        biased, running, chosen = (ring[:, 1024 * n:1024 * n + 1024] for n in range(3))
        gt, eq = ring[:, 3072:4096], ring[:, 4096:5120]
        bias_b = ring[:, 5632:5696]
        top2, grank, gkeep = (ring[:, 7744 + P * n:7744 + P * n + P] for n in range(3))
        rope_p = [[w_gu[:, 1024 * b + 512 * n:1024 * b + 512 * n + 512] for n in range(2)] for b in range(2)]
        rope_t = [w_gu[:, 2048:2560], w_gu[:, 2560:3072], w_gu[:, 7168:7680], ring[:, 6464:6976]]
        attn_f = attn[:, :, :].rearrange("p i d -> p (i d)")
        part_at = [w_gu[:, 3072:3840], w_gu[:, 3840:4608], ring[:, 5696:6464], ring[:, 6976:7744],
                   attn_f[:, 0:768], attn_f[:, 768:1536], w_gu[:, 5632:6400], w_gu[:, 6400:7168]]
        parts = [[a[:, 256 * n:256 * n + 256].bitcast(BF16) for n in range(3)] for a in part_at]
        PARTS = len(parts)
        score = w_gu[:, 4608:5632]
        slot, onehot, kept_score = arena[:, 4096:5120], arena[:, 5120:5632], arena[:, 5760:6784]
        product = [arena[:, a:a + 512].rearrange("p (k e) -> p k e", k=K) for a in (5120, 6784, 7296, 7808)]
        match = [arena[:, 256 * i:256 * i + 256].bitcast(BF16).rearrange("p (k e) -> p k e", k=K) for i in range(NT)]
        level = [ring[:, 3072 + a:3072 + a + n] for a, n in (
            (0, 512), (512, 512), (1024, 256), (1280, 256), (1536, 256), (1792, 256),
            (2048, 128), (2176, 128), (2304, 128), (2432, 128))]
        best = w_gu[:, 0:128].rearrange("p (i k) -> p i k", k=K)
        slot8 = arena[:, 5632:5760].rearrange("p (i k) -> p i k", k=K)
        chosenb = w_gu[:, 256:768].bitcast(BF16)
        glow = w_gu[:, 768:896]
        ntile, tend, tbase = (w_gu[:, 8064 + 64 * n:8128 + 64 * n] for n in range(3))
        ntile_i = w_gu[:, 8256:8320].bitcast(I32)
        ones64 = sb("ones64", [P, E])
        wsum = sb("wsum", [P, 2, NT])
        x_in = [ring[:, 512 * n:512 * n + 512] for n in range(UNROLL)]
        x_T = [ring[:, 2048 + 512 * n:2560 + 512 * n] for n in range(2)]
        gated = [ring[:, 3072 + 256 * n:3328 + 256 * n] for n in range(2)]
        h_sb = [ring[:, 3584 + 256 * n:3840 + 256 * n] for n in range(2)]
        h_T = [ring[0:F, 4096 + 512 * n:4608 + 512 * n] for n in range(2)]
        Y_ROOM = 5120
        y_sb = [ring[:, Y_ROOM + 512 * n:Y_ROOM + 512 * n + 512] for n in range(2)]
        gathered = [w_gu[:, 2 * CH + K * P * n:2 * CH + K * P * (n + 1)].rearrange("p (j d) -> p j d", j=K)
                    for n in range(GATHERS)]
        a_T, o_out = w_gu[:, 0:CH], w_gu[:, CH:2 * CH]

        def c_(name):
            return cst[:, CONST_AT[name]:CONST_AT[name] + CONST_W[CONST.index(name)]]

        s_x, s_c, s_w, s_cs, s_bias, s_rows = (sem(n) for n in ("s_x", "s_c", "s_w", "s_cs", "s_bias", "s_rows"))
        s_zrest = [sem(f"s_zrest{b}") for b in range(2)]
        s_zset, s_zfill, s_cb, s_qzero, s_vset = (sem(n) for n in ("s_zset", "s_zfill", "s_cb", "s_qzero", "s_vset"))
        s_var, s_std, s_xn, s_xt, s_xtc, s_wt, s_wtc = (sem(n) for n in (
            "s_var", "s_std", "s_xn", "s_xt", "s_xtc", "s_wt", "s_wtc"))
        s_lg, s_sig, s_chosen, s_rank, s_idx, s_own = (sem(n) for n in (
            "s_lg", "s_sig", "s_chosen", "s_rank", "s_idx", "s_own"))
        s_ownd, s_ownr, s_disp, s_shx = (sem(n) for n in ("s_ownd", "s_ownr", "s_disp", "s_shx"))
        s_rp, s_rope, s_hi, s_r1, s_mid, s_part = (sem(n) for n in ("s_rp", "s_rope", "s_hi", "s_r1", "s_mid", "s_part"))
        s_prt = [sem(f"s_prt{b}") for b in range(PARTS)]
        s_v, s_vc, s_ready = sem("s_v"), sem("s_vc"), sem("s_ready")
        s_grp = [sem(f"s_grp{b}") for b in range(2)]
        s_wgu, s_wdn = sem("s_wgu"), [sem(f"s_wdn{b}") for b in range(2)]
        s_m, s_nmb, s_nmt = (sem(n) for n in ("s_m", "s_nmb", "s_nmt"))
        s_free = [sem(f"s_free{b}") for b in range(len(RING))]
        s_shr = [sem(f"s_shr{b}") for b in range(2)]
        s_sc, s_exp, s_pv, s_vg, s_ocp, s_ot = (sem(n) for n in ("s_sc", "s_exp", "s_pv", "s_vg", "s_ocp", "s_ot"))
        s_fin = [sem(f"s_fin{b}") for b in range(UNROLL)]
        s_fout = [sem(f"s_fout{b}") for b in range(2)]
        s_fxt, s_fxc, s_fgu, s_fe, s_fh, s_fht, s_fhc, s_fy, s_fyc = (sem(n) for n in (
            "s_fxt", "s_fxc", "s_fgu", "s_fe", "s_fh", "s_fht", "s_fhc", "s_fy", "s_fyc"))
        s_gat, s_shy = [sem(f"s_gat{b}") for b in range(GATHERS)], sem("s_shy")
        s_comb, s_pr, s_out = (sem(n) for n in ("s_comb", "s_pr", "s_out"))
        s_kept = sem("s_kept")
        s_at, s_match, s_prod, s_weigh = (sem(n) for n in ("s_at", "s_match", "s_prod", "s_weigh"))
        s_dv = sem("s_dv")

        STEPS = plan()
        taken, n = {}, 0
        for s in STEPS:
            taken[s] = n
            n += s[0] in ("block", "shift", "norm", "project", "emit")

        def ring_place(s):
            return RING[taken[s] % len(RING)], taken[s] // len(RING)

        def ring_sem(bank):
            return s_free[RING.index(bank)]

        def wait_ring(eng, s):
            for a in range(len(RING)):
                wait(eng, s_free[a], (taken[s] + len(RING) - 1 - a) // len(RING))

        def expert_steps(eng, fstep):
            for first in (0, UNROLL):
                for b in range(UNROLL):
                    fstep(first, b)
            with eng.Fori(2 * UNROLL, FSTEPS, UNROLL) as first:
                for b in range(UNROLL):
                    fstep(first, b)
            for b in range(3):
                fstep(FSTEPS, b)

        def stage(first, b, d):
            if isinstance(first, int) and not 0 <= first + b - d < FSTEPS:
                return None
            return b - d, (b - d) % UNROLL

        def zero_slots(eng, n):
            rows = SLOT_TILES * P // ZFILLS
            return eng.dma_start(x_slots[rows * n:rows * n + rows, :].rearrange("(k p r) d -> p k (r d)", p=P, r=4),
                                 zrow[:, :].rearrange("p (a n) -> p a n", a=1).broadcast_to(
                                     [P, SLOT_TILES // 4 // ZFILLS, 512]))

        block = ctx.enter_context(nc.Block())

        @block.sync
        def _(sp):
            sp.dma_start(acc[:, :, :], x_v).then_inc(s_x, 16)
            sp.dma_start(cst[:, :], consts).then_inc(s_c, 16)
            for n, w in enumerate((wq, wk, wv, wo)):
                sp.dma_start(wraw[:, n * P:n * P + P], w).then_inc(s_w, 16)
            sp.dma_start(wraw[0:E, 4 * P:5 * P], gate_w).then_inc(s_w, 16)
            sp.dma_start(bias_b, gate_bias.rearrange("(a e) -> a e", a=1).broadcast_to([P, E])).then_inc(s_bias, 16)
            sp.dma_start(cos_s, cosT).then_inc(s_cs, 16)
            sp.dma_start(sin_s, sinT).then_inc(s_cs, 16)
            sp.wait_ge(s_zset, 2)
            for n in range(EARLY_ZFILLS):
                zero_slots(sp, n).then_inc(s_zfill, 16)
            zb = zrow[0:H, :].bitcast(BF16).rearrange("p (a n) -> p a n", a=1)
            for rows, r0 in ((q_rows, SHIFT_ROW), (k_rows, SHIFT_ROW + 3)):
                sp.dma_start(rows[:, r0:HALF, :].rearrange("h r (a n) -> h (r a) n", n=1024),
                             zb.broadcast_to([H, 2 * (HALF - r0), 1024])).then_inc(s_rows, 16)
            for r in range(3):
                sp.dma_start(k_rows[:, SHIFT_ROW + r, :].rearrange("h (a n) -> h a n", n=P),
                             onesb[0:H, :].rearrange("p (a n) -> p a n", a=1).broadcast_to([H, T // P, P])
                             ).then_inc(s_rows, 16)
            for n in range(2 * NC):
                z, c = n // NC, n % NC
                sp.wait_ge(s_part, n + 1)
                rows, part = ((k_rows, K_PART), (q_rows, Q_PART))[z]
                for g in range(PRODUCTS):
                    sp.dma_start(rows[:, DH * g:DH * g + DH, CH * c:CH * c + CH], parts[n % PARTS][part[g]]
                                 ).then_inc(s_prt[n % PARTS], 16)
            sp.wait_ge(s_rows, 16 * 5)
            for b in range(PARTS):
                sp.wait_ge(s_prt[b], 16 * PRODUCTS * len(range(b, 2 * NC, PARTS)))
            sp.wait_ge(s_qzero, 2)

            def load_group(g):
                for hh in range(HG):
                    r0 = HALF * (hh % 2)
                    for dst, rows, at in ((qs, q_rows, (HG * (g % 2) + hh) * T),
                                          (ks, k_rows, (HG // 2 * (g % 2) + hh // 2) * T)):
                        sp.dma_start(dst[r0:r0 + HALF, at:at + T], rows[HG * g + hh]).then_inc(s_grp[g % 2], 16)

            load_group(0)
            load_group(1)
            sp.wait_ge(s_own, 2)
            for col in range(2):
                sp.dma_start(owner_d[P * col:P * col + P].rearrange("(p a) -> p a", a=1), own_i[:, col:col + 1]
                             ).then_inc(s_ownd, 16)
            sp.wait_ge(s_ownd, 32)
            sp.dma_start(owner[0:1, 0:SLOT_TILES], owner_d[0:SLOT_TILES].rearrange("(a k) -> a k", a=1)
                         ).then_inc(s_ownr, 16)
            sp.dma_start(x_slots[SLOT_TILES * P:XT_TILES * P, :].rearrange("(i p) d -> p i d", p=P), xn[:, :, :]
                         ).then_inc(s_shx, 16)
            def step(s):
                kind, n = s
                if kind == "shift":
                    g, c = CHUNKS[n]
                    bank, used = ring_place(s)
                    sp.wait_ge(ring_sem(bank), used + 1)
                    for hh in range(HG):
                        r0, at = HALF * (hh % 2) + SHIFT_ROW, (HG * (g % 2) + hh) * T + CH * c
                        sp.dma_start(qs[r0:r0 + 3, at:at + CH], shiftT[3 * hh:3 * hh + 3, n % 2, :]
                                     ).then_inc(s_shr[n % 2], 16)
                elif kind == "load":
                    sp.wait_ge(s_sc, UNITS_G * (n - 1))
                    sp.wait_ge(s_grp[n % 2], 16 * 2 * HG * (n // 2))
                    load_group(n)
                elif kind == "emit":
                    bank, used = ring_place(s)
                    sp.wait_ge(ring_sem(bank), used + 1)
                    c = CHUNKS[n][1]
                    sp.dma_start(out_v[:, 4 * c:4 * c + 4, :], o_out.rearrange("p (r d) -> p r d", r=4)
                                 ).then_inc(s_out, 16)
                elif kind == "experts":
                    sp.wait_ge(s_disp, 16 * NT * K)
                    sp.wait_ge(s_shx, 16)
                    sp.wait_ge(s_pv, QUADS_G * NG // 2 - (PROBS // HG - 1))
                    expert_steps(sp, fstep)
                    for b in range(2):
                        sp.wait_ge(s_fout[b], 16 * (FSTEPS // 2))
                    sp.dma_start(xn[:, :, :], y_slots[SLOT_TILES * P:XT_TILES * P, :].rearrange(
                        "(i p) d -> p i d", p=P)).then_inc(s_shy, 16)

            def fstep(first, b):
                if at := stage(first, b, 0):
                    off, place = at
                    wait(sp, s_fxt, first + (off - (UNROLL - 1)))
                    sp.dma_start(x_in[place].rearrange("p (r d) -> p r d", r=FB),
                                 x_slots[bass.ds(FB * P * first + FB * P * off, FB * P), :].rearrange(
                                     "(r p) d -> p r d", p=P)).then_inc(s_fin[place], 16)

            for s in STEPS:
                step(s)
            sp.wait_ge(s_out, 16 * NC)

        @block.gpsimd
        def _(pool):
            q3 = qs[:, :].rearrange("p (b m o n) -> p b m o n", b=2, m=HG // 2, o=2)
            for o in range(2):
                r0 = HALF * (1 - o)
                wait(pool, s_qzero, o)
                pool.memset(q3[r0:r0 + HALF, :, :, o, :], 0.0).then_inc(s_qzero, 1)
            pool.wait_ge(s_qzero, 2)
            pool.memset(v_g[:, :, :, DH + 1:], 0.0).then_inc(s_vset, 1)
            pool.memset(v_g[:, :, :, DH:DH + 1], 1.0).then_inc(s_vset, 1)
            for n in range(2 * NC + 1):
                if n < 2 * NC:
                    pool.wait_ge(s_rope, n + 1)
                    pool.wait_ge(s_hi, n + 1)
                    if n >= 2:
                        pool.wait_ge(s_mid, n - 1)
                        pool.wait_ge(s_part, n - 1)
                    nc.gpsimd.tensor_tensor(rope_t[2 + n % 2], rope_t[n % 2], parts[n % PARTS][0], ALU.subtract
                                            ).then_inc(s_r1, 1)
                if n >= 1:
                    a = n - 1
                    pool.wait_ge(s_mid, n)
                    pool.wait_ge(s_r1, n)
                    nc.gpsimd.tensor_tensor(parts[a % PARTS][2], rope_t[2 + a % 2], parts[a % PARTS][1], ALU.subtract
                                            ).then_inc(s_part, 1)
            pool.wait_ge(s_zset, 2)
            pool.wait_ge(s_grp[0], 16 * 2 * HG)
            for n in range(ZFILLS - EARLY_ZFILLS):
                wait(pool, s_zrest[n % 2], 16 * (n // 2))
                zero_slots(pool, EARLY_ZFILLS + n).then_inc(s_zrest[n % 2], 16)
            pool.wait_ge(s_xn, NT)
            pool.wait_ge(s_idx, 1)
            pool.wait_ge(s_zfill, 16 * EARLY_ZFILLS)
            for b in range(2):
                pool.wait_ge(s_zrest[b], 16 * len(range(b, ZFILLS - EARLY_ZFILLS, 2)))
            pool.wait_ge(s_ready, 1)
            pool.wait_ge(s_kept, 1)
            for b in range(PARTS):
                pool.wait_ge(s_prt[b], 16 * PRODUCTS * len(range(b, 2 * NC, PARTS)))
            w_gu3 = w_gu[:, :].rearrange("p (e f) -> p e f", e=E + 1)
            for w_s, at in ((ws_gate, 0), (ws_up, F)):
                pool.dma_start(w_gu3[:, E, at:at + F], w_s).then_inc(s_wgu, 16)
            for i in range(NT):
                e0, e1 = E // NT * i, E // NT * (i + WGAP)
                for w, at in ((we_gate, 0), (we_up, F)) if i % WGAP == 0 else ():
                    pool.dma_start(w_gu3[:, e0:e1, at:at + F], w[e0:e1].rearrange("e d f -> d e f")).then_inc(s_wgu, 16)
                for j in range(K):
                    pool.indirect_dma_start(x_slots, bass.IndirectOffsetOnAxis(ap=idx[:, i, j:j + 1], axis=0),
                                            xn[:, i, :], None).then_inc(s_disp, 16)
            for i in range(NT):
                pool.wait_ge(s_match, i + 1)
                wait(pool, s_weigh, i - len(product) + 1)
                nc.gpsimd.tensor_tensor(product[i % len(product)], match[i], kept_score.rearrange(
                    "p (i e) -> p i e", e=E)[:, i:i + 1, :].broadcast_to([P, K, E]), ALU.mult).then_inc(s_prod, 1)
            pool.wait_ge(s_weigh, NT)
            pool.dma_start(w_dn[:, E * P:], ws_down).then_inc(s_wdn[0], 16)
            for n in range(WLOADS):
                e0, e1 = E // WLOADS * n, E // WLOADS * (n + 1)
                wait(pool, s_wdn[n % 2], 16 * (n // 2 + (n % 2 == 0)))
                pool.dma_start(w_dn[:, P * e0:P * e1].rearrange("f (e d) -> f e d", e=e1 - e0),
                               we_down[e0:e1].rearrange("e f d -> f e d")).then_inc(s_wdn[n % 2], 16)

            def fstep(first, b):
                if at := stage(first, b, 3):
                    off, place = at
                    pool.wait_ge(s_fyc, first + (off + 1))
                    pool.dma_start(y_slots[bass.ds(FB * P * first + FB * P * off, FB * P), :].rearrange(
                        "(r p) d -> p r d", p=P), y_sb[place % 2].rearrange("p (r d) -> p r d", r=FB)
                                   ).then_inc(s_fout[place % 2], 16)

            expert_steps(pool, fstep)
            pool.wait_ge(s_disp, 16 * NT * K)
            pool.wait_ge(s_shx, 16)
            for b in range(2):
                pool.wait_ge(s_fout[b], 16 * (FSTEPS // 2))
            for a, i in enumerate(TILES):
                wait(pool, s_comb, a - GATHERS + 1)
                for j in range(K):
                    pool.indirect_dma_start(gathered[a % GATHERS][:, j, :], None, y_slots[0:XT_TILES * P, :],
                                            bass.IndirectOffsetOnAxis(ap=idx[:, i, j:j + 1], axis=0)
                                            ).then_inc(s_gat[a % GATHERS], 16)

        @block.scalar
        def _(act):
            act.wait_ge(s_cb, 5)
            act.wait_ge(s_var, 1)
            nc.scalar.activation(std[:, 0, :], mv[:, :, 1], ACT.Sqrt, bias=epsc[:, 0:1]).then_inc(s_std, 1)
            act.wait_ge(s_wt, 1)
            nc.scalar.copy(wT[:, 0:256], ps[:, 0, 0:256]).then_inc(s_wtc, 1)
            act.wait_ge(s_wt, 2)
            nc.scalar.copy(wT[:, 256:512], ps[:, 1, 0:256]).then_inc(s_wtc, 1)
            act.wait_ge(s_wt, 3)
            nc.scalar.copy(wT[:, 512:704], ps[:, 2, 0:192]).then_inc(s_wtc, 1)
            nc.scalar.copy(woT[:, :], ps[:, 2, 256:384]).then_inc(s_wtc, 1)
            for c in range(NC):
                act.wait_ge(s_xt, c + 1)
                nc.scalar.copy(xnT[:, CH * c:CH * c + CH], ps[:, 3 + c, :]).then_inc(s_xtc, 1)
            for n in range(2 * NC + 1):
                if n == 2 * NC - 2:
                    for b in range(2):
                        act.wait_ge(s_lg, b + 1)
                        nc.scalar.activation(score[:, 512 * b:512 * b + 512], ps[:, b, :], ACT.Sigmoid
                                             ).then_inc(s_sig, 1)
                if n < 2 * NC:
                    act.wait_ge(s_rope, n + 1)
                    if n >= PARTS:
                        act.wait_ge(s_prt[n % PARTS], 16 * PRODUCTS * (n // PARTS))
                    nc.scalar.copy(parts[n % PARTS][0], rope_t[n % 2]).then_inc(s_hi, 1)
                if n >= 1:
                    act.wait_ge(s_r1, n)
                    nc.scalar.copy(parts[(n - 1) % PARTS][1], rope_t[2 + (n - 1) % 2]).then_inc(s_mid, 1)
            for c in range(NC):
                act.wait_ge(s_v, c + 1)
                nc.scalar.copy(v_all[:, 4 * c:4 * c + 4, :].rearrange("p i d -> p (i d)"), ps[:, 7 - c % 2, :]
                               ).then_inc(s_vc, 1)
            act.wait_ge(s_v, NC)
            nc.scalar.copy(kept_score, score).then_inc(s_kept, 1)
            act.wait_ge(s_ready, 1)
            act.wait_ge(s_vset, 2)

            def step(s):
                kind, n = s
                if kind == "unit":
                    w = CH - unit_of(n)[-1]
                    act.wait_ge(s_sc, n + 1)
                    wait(act, s_pv, (n - PROBS) // HG + 1)
                    if n == UNITS_G * NG // 2 + Y_ROOM // CH:
                        for b in range(2):
                            act.wait_ge(s_fout[b], 16 * (FSTEPS // 2))
                    nc.scalar.activation(probs[:, n % PROBS, 0:w], ps[:, n % SCORES, 0:w], ACT.Exp,
                                         scale=float(DH) ** -0.5).then_inc(s_exp, 1)
                elif kind == "values":
                    wait(act, s_pv, QUADS_G * n)
                    nc.scalar.copy(v_g[:, :, :, 0:DH], v_all[:, :, HG * DH * n:HG * DH * (n + 1)].rearrange(
                        "p i (h d) -> p i h d", h=HG)).then_inc(s_vg, 1)
                elif kind == "o_copy":
                    act.wait_ge(s_pv, END[n] // HG)
                    wait(act, s_ot, n)
                    nc.scalar.copy(o_sb[:, :], ps[:, O_BANK, :]).then_inc(s_ocp, 1)
                elif kind == "project":
                    act.wait_ge(s_at, n % NC + 1)
                    wait(act, s_pr, n % NC)
                    bank = ring_place(s)[0]
                    nc.scalar.copy(a_T, ps[:, bank, :]).then_inc(ring_sem(bank), 1)
                elif kind == "experts":
                    experts()

            def experts():
                def fstep(first, b):
                    if at := stage(first, b, 0):
                        off, place = at
                        act.wait_ge(s_fxt, first + (off + 1))
                        wait(act, s_fgu, first + (off - 1))
                        nc.scalar.copy(x_T[place % 2], ps[:, place % 2, :]).then_inc(s_fxc, 1)
                    if at := stage(first, b, 1):
                        off, place = at
                        act.wait_ge(s_fgu, first + (off + 1))
                        wait(act, s_fh, first + (off - 1))
                        gate = ps[:, 2 + place % 2, :].rearrange("p (r f) -> p r f", r=FB)[:, :, 0:F]
                        nc.scalar.activation(gated[place % 2].rearrange("p (r f) -> p r f", r=FB), gate, ACT.Silu
                                             ).then_inc(s_fe, 1)
                    if at := stage(first, b, 2):
                        off, place = at
                        act.wait_ge(s_fht, first + (off + 1))
                        wait(act, s_fy, first + (off - 1))
                        for o in range(2):
                            nc.scalar.copy(h_T[place % 2][:, 2 * P * o:2 * P * o + 2 * P],
                                           ps[F * o:F * o + F, 4 + place % 2, 0:2 * P]).then_inc(s_fhc, 1)

                expert_steps(act, fstep)

            for s in STEPS:
                step(s)

        @block.vector
        def _(dve):
            chain = [0]

            summed, split_at = [0], [0]

            def link(ins, later=False):
                chain[0] = chain[0] + 1
                ins.then_inc(s_dv, 1)
                if not later:
                    dve.wait_ge(s_dv, chain[0])

            V = nc.vector
            V.memset(zrow[:, :], 0.0).then_inc(s_zset, 1)
            V.memset(onesb[:, :], 1.0).then_inc(s_zset, 1)
            V.memset(epsc[:, :], EPS).then_inc(s_cb, 1)
            V.memset(owner[:, :], E * P).then_inc(s_cb, 1)
            link(V.memset(ones64[:, :], 1.0))
            dve.wait_ge(s_x, 16)
            for i in range(NT):
                last = V.bn_stats(stats[:, i, :], acc[:, i, :])
            link(last)
            for i in range(NT):
                last = V.bn_aggr(mv[:, i, :], stats[:, i, :])
            last.then_inc(s_var, 1)
            dve.wait_ge(s_c, 16)
            for dst, src in ((identb, "ident"), (maskqb, "mask_q"), (maskkb, "mask_k")):
                last = V.tensor_copy(dst[:, :], c_(src))
            last.then_inc(s_cb, 1)
            V.tensor_copy(ltrib[:, :], c_("ltri")).then_inc(s_cb, 1)
            V.memset(nmb[:, :, :], 0.0).then_inc(s_cb, 1)
            dve.wait_ge(s_std, 1)
            link(V.reciprocal(std[:, 1, :], std[:, 0, :]))
            for i in range(NT):
                V.tensor_scalar(xn[:, i, :], acc[:, i, :], mv[:, i, 0:1], std[:, 1, i:i + 1],
                                ALU.subtract, ALU.mult).then_inc(s_xn, 1)

            dve.wait_ge(s_cs, 32)
            for n in range(2 * NC):
                c, b = n % NC, 2 + 2 * (n % 2)
                t0, t1 = rope_p[n % 2]
                dve.wait_ge(s_rp, n + 1)
                wait(dve, s_rope, n - 1)
                V.tensor_tensor(t0, ps[:, b, :], cos_s[:, CH * c:CH * c + CH], ALU.mult)
                link(V.tensor_tensor(t1, ps[:, b + 1, :], sin_s[:, CH * c:CH * c + CH], ALU.mult))
                if n >= 2:
                    dve.wait_ge(s_hi, n - 1)
                    dve.wait_ge(s_r1, n - 1)
                V.tensor_tensor(rope_t[n % 2], t0, t1, ALU.add).then_inc(s_rope, 1)

            def ie(a, n=E):
                return a.rearrange("p (i e) -> p i e", e=n)

            dve.wait_ge(s_sig, 2)
            dve.wait_ge(s_bias, 16)
            link(V.tensor_tensor(ie(biased), ie(score), bias_b.rearrange("p (a e) -> p a e", a=1)
                                 .broadcast_to([P, NT, E]), ALU.add))
            hi1, lo1, hi2, t2, u2, lo2, hi3, t3, u3, lo3 = level
            b8, h4, l4 = ie(biased, 8), ie(hi1, 4), ie(lo1, 4)
            V.tensor_tensor(h4, b8[:, :, 0:4], b8[:, :, 4:8], ALU.max)
            link(V.tensor_tensor(l4, b8[:, :, 0:4], b8[:, :, 4:8], ALU.min))
            V.tensor_tensor(ie(t2, 2), h4[:, :, 0:2], h4[:, :, 2:4], ALU.min)
            V.tensor_tensor(ie(u2, 2), l4[:, :, 0:2], l4[:, :, 2:4], ALU.max)
            V.tensor_tensor(ie(hi2, 2), h4[:, :, 0:2], h4[:, :, 2:4], ALU.max)
            link(V.memset(std[:, 0, :], 0.0))
            link(V.tensor_tensor(lo2, t2, u2, ALU.max))
            h2, l2 = ie(hi2, 2), ie(lo2, 2)
            V.tensor_tensor(ie(t3, 1), h2[:, :, 0:1], h2[:, :, 1:2], ALU.min)
            V.tensor_tensor(ie(u3, 1), l2[:, :, 0:1], l2[:, :, 1:2], ALU.max)
            V.tensor_tensor(ie(hi3, 1), h2[:, :, 0:1], h2[:, :, 1:2], ALU.max)
            link(V.memset(std[:, 0, :], 0.0))
            link(V.tensor_tensor(lo3, t3, u3, ALU.max))
            link(V.tensor_tensor(top2, hi3, lo3, ALU.add))
            other = top2.rearrange("p (i a g) -> p i a g", a=1, g=G).broadcast_to([P, NT, G, G])
            own = top2.rearrange("p (i g a) -> p i g a", a=1, g=G).broadcast_to([P, NT, G, G])
            gt4, eq4 = (a.rearrange("p (i g o) -> p i g o", g=G, o=G) for a in (gt, eq))
            V.tensor_tensor(eq4, other, own, ALU.is_equal)
            link(V.tensor_tensor(gt4, other, own, ALU.is_gt))
            link(V.tensor_tensor(ie(eq), ie(eq), c_("tri").rearrange("p (a e) -> p a e", a=1)
                                 .broadcast_to([P, NT, G * G]), ALU.mult))
            link(V.tensor_tensor(gt, gt, eq, ALU.add))
            link(V.tensor_reduce(grank, gt4, AX.X, ALU.add))
            link(V.tensor_scalar(gkeep, grank, float(TG), None, ALU.is_lt))
            V.tensor_scalar(glow, gkeep, -1.0, -LOW, ALU.add, ALU.mult)
            keep8 = gkeep.rearrange("p (g a) -> p g a", a=1).broadcast_to([P, NT * G, 8])
            low8 = glow.rearrange("p (g a) -> p g a", a=1).broadcast_to([P, NT * G, 8])
            link(V.tensor_tensor(ie(running, 8), b8, keep8, ALU.mult))
            link(V.tensor_tensor(ie(running, 8), ie(running, 8), low8, ALU.add))
            for i in range(NT):
                last = V.max(best[:, i, :], ie(running)[:, i, :])
            link(last)
            for i in range(NT):
                last = V.match_replace(ie(chosen)[:, i, :], best[:, i, :], ie(running)[:, i, :], MARK)
            link(last)
            link(V.tensor_scalar(chosen, chosen, 3.2e38, None, ALU.is_ge))
            V.tensor_copy(chosenb, chosen).then_inc(s_chosen, 1)
            dve.wait_ge(s_rank, 1)
            link(V.tensor_scalar(ntile_i, ps[:, 7, 0:E], float(P - 1), None, ALU.add))
            link(V.tensor_scalar(ntile_i, ntile_i, 7, None, ALU.logical_shift_right))
            link(V.tensor_copy(ntile, ntile_i))
            link(V.tensor_tensor_scan(tend, ones64[:, :], ntile, 0.0, ALU.mult, ALU.add))
            link(V.tensor_tensor(tbase, tend, ntile, ALU.subtract))
            link(V.tensor_scalar(tbase, tbase, float(P), 1.0, ALU.mult, ALU.add))
            base16 = tbase.rearrange("p (a e) -> p a e", a=1).broadcast_to([P, NT // 2, E])
            for b in range(2):
                dve.wait_ge(s_rank, b + 2)
                last = V.tensor_tensor(ie(slot)[:, 8 * b:8 * b + 8, :], ps[:, b, :].rearrange("p (i e) -> p i e", e=E),
                                       base16, ALU.add)
            link(last)
            link(V.tensor_tensor(slot, slot, chosen, ALU.mult))
            for i in range(NT):
                last = V.max(slot8[:, i, :], ie(slot)[:, i, :])
            link(last)
            V.tensor_scalar(idx[:, :, :], slot8, -1.0, None, ALU.add).then_inc(s_idx, 1)
            for col in range(2):
                V.tensor_scalar(onehot[:, E * col:E * col + E], tend, c_("kid")[:, col:col + 1], None, ALU.is_le)
            link(V.memset(std[:, 0, :], 0.0))
            link(V.memset(std[:, 0, :], 0.0))
            link(V.tensor_reduce(own_f[:, :], onehot[:, 0:2 * E].rearrange("p (c e) -> p c e", c=2), AX.X, ALU.add))
            link(V.tensor_scalar(own_f[:, :], own_f[:, :], float(E - 1), float(P), ALU.min, ALU.mult))
            V.tensor_copy(own_i[:, :], own_f[:, :]).then_inc(s_own, 2)

            V.memset(std[:, 0, :], 0.0).then_inc(s_ready, 1)

            def step(s):
                kind, n = s
                if kind == "block":
                    m, _, _, hh, r, kb, w = block_of(n)
                    dve.wait_ge(s_m, n + 1)
                    bank = ring_place(s)[0]
                    V.tensor_reduce(mp[:, m % 2, HG * r + hh, kb:kb + 1], ps[:, bank, 0:w], AX.X, ALU.max
                                    ).then_inc(ring_sem(bank), 1)
                elif kind == "max_done":
                    m, k = n
                    if k == 0:
                        wait_ring(dve, s)
                        ins = V.tensor_reduce(nm[:, :], mp[:, m % 2, :, 0:CHUNKS[m][1] + 1], AX.X, ALU.max, negate=True)
                    else:
                        dve.wait_ge(s_dv, split_at[0])
                    if k == 1:
                        wait(dve, s_nmt, m)
                        ins = V.tensor_copy(nmb[:, :, 0], nm[:, :])
                    elif k == 2:
                        ins = V.tensor_tensor(nmr[:, 0, :], nm[:, :], nmb[:, :, 0], ALU.subtract)
                    elif k == 3:
                        ins = V.tensor_copy(nmb[:, :, 1], nmr[:, 0, :])
                    elif k == 4:
                        V.tensor_tensor(nmb[:, :, 2], nmr[:, 0, :], nmb[:, :, 1], ALU.subtract).then_inc(s_nmb, 1)
                    if k < SPLITS - 1:
                        link(ins, later=True)
                        split_at[0] = chain[0]
                elif kind == "match":
                    V.tensor_tensor(match[n], ie(slot)[:, n:n + 1, :].broadcast_to([P, K, E]),
                                    slot8[:, n, :].rearrange("p (k a) -> p k a", a=1).broadcast_to([P, K, E]),
                                    ALU.is_equal).then_inc(s_match, 1)
                elif kind == "weigh":
                    dve.wait_ge(s_prod, n + 1)
                    V.tensor_reduce(pos_w[:, n, :], product[n % len(product)], AX.X, ALU.add).then_inc(s_weigh, 1)
                elif kind == "shift":
                    dve.wait_ge(s_nmt, n + 1)
                    wait(dve, s_shr[n % 2], 64 * (n // 2))
                    bank = ring_place(s)[0]
                    V.tensor_copy(shiftT[:, n % 2, :], ps[0:3 * HG, bank, 0:CH // 2].bitcast(BF16)
                                  ).then_inc(ring_sem(bank), 1)
                elif kind == "norm":
                    g, c = CHUNKS[n]
                    dve.wait_ge(s_ot, n + 1)
                    bank = ring_place(s)[0]
                    o4 = ps[:, bank, :].rearrange("p (a m) -> p a m", m=32)
                    link(V.reciprocal(rden[:, :].rearrange("p (a m) -> p a m", m=1), o4[:, :, DH:DH + 1]))
                    a4 = attn[:, 4 * c:4 * c + 4, HG * DH * g:HG * DH * (g + 1)]
                    V.tensor_tensor(a4.rearrange("p r (h d) -> p r h d", h=HG),
                                    ps[:, bank, :].rearrange("p (r h m) -> p r h m", r=4, h=HG)[:, :, :, 0:DH],
                                    rden[:, :].rearrange("p (r h m) -> p r h m", r=4, m=1).broadcast_to(
                                        [P, 4, HG, DH]), ALU.mult).then_inc(ring_sem(bank), 1)
                elif kind == "combine":
                    i, j = n
                    a = TILES.index(i)
                    if j == 0:
                        dve.wait_ge(s_shy, 16)
                        link(V.tensor_tensor(acc[:, i, :], acc[:, i, :], xn[:, i, :], ALU.add), later=True)
                    else:
                        if j == 1:
                            dve.wait_ge(s_gat[a % GATHERS], 16 * K * (a // GATHERS + 1))
                        dve.wait_ge(s_dv, summed[0])
                        ins = V.scalar_tensor_tensor(acc[:, i, :], gathered[a % GATHERS][:, j - 1, :],
                                                     pos_w[:, i, j - 1:j], acc[:, i, :], ALU.mult, ALU.add)
                        if j < K:
                            link(ins, later=True)
                        else:
                            ins.then_inc(s_comb, 1)
                    summed[0] = chain[0]
                elif kind == "emit":
                    c = CHUNKS[n][1]
                    dve.wait_ge(s_pr, n % NC + 1)
                    dve.wait_ge(s_comb, 4 * (n % NC + 1))
                    wait(dve, s_out, 16 * (n % NC))
                    bank = ring_place(s)[0]
                    V.tensor_tensor(o_out, ps[:, bank, :], acc[:, 4 * c:4 * c + 4, :].rearrange(
                        "p r d -> p (r d)"), ALU.add).then_inc(ring_sem(bank), 1)
                elif kind == "experts":
                    dve.wait_ge(s_weigh, NT)
                    link(V.tensor_reduce(wsum[:, 0, :], pos_w[:, :, :], AX.X, ALU.add))
                    link(V.tensor_scalar(wsum[:, 0, :], wsum[:, 0, :], 1e-20, None, ALU.add))
                    link(V.reciprocal(wsum[:, 1, :], wsum[:, 0, :]))
                    link(V.scalar_tensor_tensor(pos_w[:, :, :], pos_w[:, :, :], ROUTE_SCALE,
                                                wsum[:, 1, :].rearrange("p (i a) -> p i a", a=1).broadcast_to(
                                                    [P, NT, K]), ALU.mult, ALU.mult))
                    experts()

            def experts():
                def fstep(first, b):
                    if at := stage(first, b, 1):
                        off, place = at
                        dve.wait_ge(s_fe, first + (off + 1))
                        wait(dve, s_fht, first + (off - 1))
                        up = ps[:, 2 + place % 2, :].rearrange("p (r f) -> p r f", r=FB)[:, :, F:2 * F]
                        V.tensor_tensor(h_sb[place % 2].rearrange("p (r f) -> p r f", r=FB), up,
                                        gated[place % 2].rearrange("p (r f) -> p r f", r=FB), ALU.mult
                                        ).then_inc(s_fh, 1)
                    if at := stage(first, b, 3):
                        off, place = at
                        dve.wait_ge(s_fy, first + (off + 1))
                        wait(dve, s_fout[place % 2], 8 * first + 16 * (off // 2))
                        V.tensor_copy(y_sb[place % 2], ps[:, 6 + place % 2, :]).then_inc(s_fyc, 1)

                expert_steps(dve, fstep)

            for s in STEPS:
                step(s)

        @block.tensor
        def _(pe):
            pe.wait_ge(s_c, 16)
            pe.wait_ge(s_w, 16 * 5)
            ident = c_("ident")
            turned = cst[:, CONST_AT["ident"]:CONST_AT["ident"] + 2 * P]
            for n in range(2):
                pe.matmul(ps[:, n, 0:2 * P], wraw[:, n * P:n * P + P], turned, start=True, stop=True).then_inc(s_wt, 1)
            pe.transpose(ps[:, 2, 0:P], wraw[:, 2 * P:3 * P], ident)
            pe.transpose(ps[:, 2, P:P + E], wraw[0:E, 4 * P:5 * P], ident[0:E, 0:E])
            pe.transpose(ps[:, 2, 2 * P:3 * P], wraw[:, 3 * P:4 * P], ident).then_inc(s_wt, 1)
            for i in range(NT):
                pe.wait_ge(s_xn, i + 1)
                last = pe.transpose(ps[:, 3 + i // 4, P * (i % 4):P * (i % 4) + P], xn[:, i, :], ident)
                if i % 4 == 3:
                    last.then_inc(s_xt, 1)
            pe.wait_ge(s_wtc, 4)
            def rope(n):
                z, c = 2 * P * (1 - n // NC), n % NC
                pe.wait_ge(s_xtc, 1 if n == 0 else 3 if n < 3 else NC)
                if n >= 2:
                    pe.wait_ge(s_rope, n - 1)
                b = 2 + 2 * (n % 2)
                pe.matmul(ps[:, b, :], wT[:, z:z + P], xnT[:, CH * c:CH * c + CH], start=True, stop=True)
                pe.matmul(ps[:, b + 1, :], wT[:, z + P:z + 2 * P], xnT[:, CH * c:CH * c + CH], start=True, stop=True
                          ).then_inc(s_rp, 1)

            for n in range(2 * NC):
                rope(n)
            for i in range(NT):
                pe.wait_ge(s_xtc, i // 4 + 1)
                last = pe.matmul(ps[:, i // 8, E * (i % 8):E * (i % 8) + E], xnT[:, P * i:P * i + P],
                                 wT[:, 5 * P:5 * P + E], start=True, stop=True)
                if i % 8 == 7:
                    last.then_inc(s_lg, 1)
            for c in range(NC):
                if c >= 2:
                    pe.wait_ge(s_vc, c - 1)
                for r in range(4):
                    i = 4 * c + r
                    last = pe.matmul(ps[:, 7 - c % 2, P * r:P * r + P], xnT[:, P * i:P * i + P],
                                     wT[:, 4 * P:5 * P], start=True, stop=True)
                last.then_inc(s_v, 1)
            pe.wait_ge(s_chosen, 1)
            pe.wait_ge(s_cb, 5)
            pe.wait_ge(s_zset, 2)
            pe.wait_ge(s_sig, 2)
            pe.wait_ge(s_vc, NC)
            ch3 = chosenb.rearrange("p (i e) -> p i e", e=E)
            for i in range(NT):
                last = pe.matmul(ps[:, 7, 0:E], onesb[:, :], ch3[:, i, :], start=i == 0, stop=i == NT - 1)
            last.then_inc(s_rank, 1)
            for b in range(2):
                i0, i1 = 8 * b, 8 * b + 8
                pe.matmul(ps[:, b, :], ltrib[:, :], chosenb[:, 512 * b:512 * b + 512], start=True, stop=False)
                for j in range(i1 - 1):
                    a = max(i0, j + 1)
                    last = pe.matmul(ps[:, b, E * (a - i0):512].rearrange("p (i e) -> p i e", e=E), onesb[:, :],
                                     ch3[:, j:j + 1, :].broadcast_to([P, i1 - a, E]), start=False, stop=j == i1 - 2)
                last.then_inc(s_rank, 1)
            pe.wait_ge(s_ready, 1)

            def step(s):
                kind, n = s
                if kind == "block":
                    m, g, c, hh, r, kb, w = block_of(n)
                    if n % UNITS_G == 0:
                        pe.wait_ge(s_grp[g % 2], 16 * 2 * HG * (g // 2 + 1))
                    at, used = ring_place(s)
                    wait(pe, ring_sem(at), used)
                    bank = ps[:, at, :]
                    diag = kb == c
                    q0, k0 = (HG * (g % 2) + hh) * T + CH * c + P * r, (HG // 2 * (g % 2) + hh // 2) * T + CH * kb
                    last = pe.matmul(bank[:, 0:w], qs[:, q0:q0 + P], ks[:, k0:k0 + w], start=True, stop=not diag)
                    if diag:
                        last = pe.matmul(bank[:, w - P:w], identb[:, :], maskqb[:, :], start=False, stop=True)
                    last.then_inc(s_m, 1)
                elif kind == "unit":
                    m, g, c, hh, j, skip = unit_of(n)
                    if n == END[m] - SIZE[m]:
                        pe.wait_ge(s_shr[m % 2], 64 * (m // 2 + 1))
                    wait(pe, s_exp, n - SCORES + 1)
                    dst = ps[:, n % SCORES, 0:CH - skip]
                    diag = j >= 4 * c
                    q0, k0 = (HG * (g % 2) + hh) * T + CH * c, (HG // 2 * (g % 2) + hh // 2) * T + P * j
                    last = pe.matmul(dst, ks[:, k0:k0 + P], qs[:, q0 + skip:q0 + CH], start=True, stop=not diag)
                    if diag:
                        last = pe.matmul(dst[:, 0:P], identb[:, :], maskkb[:, :], start=False, stop=True)
                    last.then_inc(s_sc, 1)
                elif kind == "pv":
                    pe.wait_ge(s_exp, HG * n + HG)
                    m, g, c, _, j, skip = unit_of(HG * n)
                    if HG * n == END[m] - SIZE[m]:
                        wait(pe, s_ocp, m)
                    if n % QUADS_G == 0:
                        pe.wait_ge(s_vg, g + 1)
                    for hh in range(HG):
                        last = pe.matmul(ps[32 * hh:32 * hh + 32, O_BANK, skip:CH], v_g[:, j, hh, :],
                                         probs[:, (HG * n + hh) % PROBS, 0:CH - skip], start=j == 0, stop=j == 4 * c + 3)
                    last.then_inc(s_pv, 1)
                elif kind == "shift":
                    pe.wait_ge(s_nmb, n + 1)
                    bank, used = ring_place(s)
                    wait(pe, ring_sem(bank), used)
                    xb = ps[0:3 * HG, bank, 0:CH // 2].bitcast(BF16)
                    for r in range(4):
                        last = pe.transpose(xb[:, P * r:P * r + P], nmb[:, HG * r:HG * r + HG, :].rearrange(
                            "p h t -> p (h t)"), identb[:, :])
                    last.then_inc(s_nmt, 1)
                elif kind == "norm":
                    pe.wait_ge(s_ocp, n + 1)
                    bank, used = ring_place(s)
                    wait(pe, ring_sem(bank), used)
                    for r in range(4):
                        last = pe.transpose(ps[:, bank, P * r:P * r + P], o_sb[:, P * r:P * r + P], ident)
                    last.then_inc(s_ot, 1)
                elif kind == "project":
                    bank, used = ring_place(("norm", n))
                    pe.wait_ge(ring_sem(bank), used + 1)
                    bank, used = ring_place(s)
                    pe.wait_ge(ring_sem(bank), used)
                    for r in range(4):
                        last = pe.transpose(ps[:, bank, P * r:P * r + P], attn[:, 4 * CHUNKS[n][1] + r, :], ident)
                    last.then_inc(s_at, 1)
                elif kind == "emit":
                    bank, used = ring_place(("project", n))
                    pe.wait_ge(ring_sem(bank), used + 1)
                    bank, used = ring_place(s)
                    pe.wait_ge(ring_sem(bank), used)
                    for r in range(4):
                        last = pe.matmul(ps[:, bank, P * r:P * r + P], a_T[:, P * r:P * r + P], woT[:, :],
                                         start=True, stop=True)
                    last.then_inc(s_pr, 1)
                elif kind == "experts":
                    experts(s)

            def experts(s):
                pe.wait_ge(s_exp, UNITS_G * NG // 2)
                wait_ring(pe, s)
                pe.wait_ge(s_ocp, NC * NG // 2)
                pe.wait_ge(s_wgu, 16 * 2 * (NT // WGAP + 1))
                for b in range(2):
                    pe.wait_ge(s_wdn[b], 16 * (WLOADS // 2 + (b == 0)))
                pe.wait_ge(s_ownr, 16)

                def owners(first, off):
                    return nc.values_load_multi_w_load_instructions(
                        owner[0:1, bass.ds(FB * first + FB * off, FB)], engines=[mybir.EngineType.PE], min_val=0, max_val=E * P,
                        skip_runtime_bounds_check_because="VectorE caps the numbers at E")[1]

                def fstep(first, b):
                    if at := stage(first, b, 0):
                        off, place = at
                        pe.wait_ge(s_fin[place], 16 // UNROLL * first + 16 * (off // UNROLL + 1))
                        wait(pe, s_fxc, first + (off - 1))
                        for r in range(FB):
                            last = pe.transpose(ps[:, place % 2, P * r:P * r + P], x_in[place][:, P * r:P * r + P],
                                                ident)
                        last.then_inc(s_fxt, 1)
                    if at := stage(first, b, 1):
                        off, place = at
                        experts_of = owners(first, off)
                        pe.wait_ge(s_fxc, first + (off + 1))
                        wait(pe, s_fh, first + (off - 1))
                        for r, e in enumerate(experts_of):
                            last = pe.matmul(ps[:, 2 + place % 2, P * r:P * r + P], x_T[place % 2][:, P * r:P * r + P],
                                             w_gu[:, bass.ds(e, 2 * F)], start=True, stop=True)
                        last.then_inc(s_fgu, 1)
                    if at := stage(first, b, 2):
                        off, place = at
                        pe.wait_ge(s_fh, first + (off + 1))
                        wait(pe, s_fhc, 2 * first + 2 * (off - 1))
                        for r in range(FB // 2):
                            last = pe.transpose(ps[:, 4 + place % 2, P * r:P * r + P],
                                                h_sb[place % 2][:, P * r:P * r + P], ident)
                        last.then_inc(s_fht, 1)
                    if at := stage(first, b, 3):
                        off, place = at
                        experts_of = owners(first, off)
                        pe.wait_ge(s_fhc, 2 * first + 2 * (off + 1))
                        wait(pe, s_fyc, first + (off - 1))
                        for r, e in enumerate(experts_of):
                            at_r = 2 * (r % 2) + r // 2
                            last = pe.matmul(ps[:, 6 + place % 2, P * r:P * r + P], h_T[place % 2][
                                :, P * at_r:P * at_r + P], w_dn[:, bass.ds(e, P)], start=True, stop=True)
                        last.then_inc(s_fy, 1)

                expert_steps(pe, fstep)
                pe.wait_ge(s_fyc, FSTEPS)

            for s in STEPS:
                step(s)


def tables():
    f = np.float32
    turn = np.zeros((P, P), f)
    for i in range(0, P, 2):
        turn[i + 1, i], turn[i, i + 1] = -1.0, 1.0
    a = np.arange(P)
    part = {
        "ident": np.eye(P, dtype=f),
        "rot": turn,
        "ltri": (a[:, None] < a[None, :]).astype(f),
        "mask_q": np.where(a[None, :] > a[:, None], f(NEG), f(0)),
        "mask_k": np.where(a[None, :] < a[:, None], f(NEG), f(0)),
        "tri": np.broadcast_to((a[None, :G] < a[:G, None]).astype(f).reshape(1, G * G), (P, G * G)),
        "kid": np.stack([a, a + P], 1).astype(f),
    }
    consts = np.ascontiguousarray(np.concatenate([part[n] for n in CONST], 1).astype(f))
    inv = f(1.0) / (f(10000.0) ** (np.arange(0, DH, 2, dtype=f) / f(DH)))
    angle = np.outer(np.arange(T, dtype=f), inv).astype(f)
    rows = np.tile(np.repeat(angle.T, 2, axis=0), (H, 1))
    return consts, np.ascontiguousarray(np.cos(rows)), np.ascontiguousarray(np.sin(rows))


_INS = ['L0_attn_x', 'L0_attn_Wq', 'L0_attn_Wk', 'L0_attn_Wv', 'L0_attn_Wo', 'L0_ffn_gate_w', 'L0_ffn_gate_bias',
        'L0_ffn_We_gate', 'L0_ffn_We_up', 'L0_ffn_We_down', 'L0_ffn_Ws_gate', 'L0_ffn_Ws_up', 'L0_ffn_Ws_down']
_OUTS = [((1, T, P), 'float32')]


def kernel(**inputs):
    import numpy as _np
    import concourse.bacc as _bacc
    from concourse import mybir as _mybir
    from concourse.bass_utils import run_bass_kernel_spmd as _run

    nc = _bacc.Bacc("TRN2", target_bir_lowering=False, num_devices=1)
    arrays, args = {}, []
    given = [(n, _np.ascontiguousarray(inputs[n])) for n in _INS] + list(zip(("consts", "cosT", "sinT"), tables()))
    for name, a in given:
        arrays[f"in_{name}_dram"] = a
        args.append(nc.dram_tensor(f"in_{name}_dram", a.shape, _mybir.dt.from_np(a.dtype), kind="ExternalInput").ap())
    for i, (shape, dtype) in enumerate(_OUTS):
        dt = _mybir.dt.from_np(_np.dtype(dtype))
        args.append(nc.dram_tensor(f"out_{i}_dram", shape, dt, kind="ExternalOutput").ap())
    build(nc, *args)
    r = _run(nc, [arrays], core_ids=[0])
    return r.results[0]["out_0_dram"]
```
